# Optimizing a Trainium2 kernel written in Bass

```python
import numpy as np
import jax
import jax.numpy as jnp

def _softmax(x, axis=-1):
    return jax.nn.softmax(x, axis=axis)

def _gelu(x):
    return jax.nn.gelu(x, approximate=True)

def _silu(x):
    return jax.nn.silu(x)

def _sigmoid(x):
    return jax.nn.sigmoid(x)

def _layernorm(x, axis=-1, eps=1e-05):
    m = jnp.mean(x, axis=axis, keepdims=True)
    v = jnp.var(x, axis=axis, keepdims=True)
    return (x - m) / jnp.sqrt(v + eps)

def _scatter_add(tgt, idx, src, axis=0):
    return tgt.at[idx].add(src)

def _segment_sum(src, seg, n):
    return jax.ops.segment_sum(src, seg, n)
kernel_name = 'mk_decoder_postln_d1_seqx_r8_8687ac'

def setup_inputs(seed: int=0):
    np.random.seed(seed)
    _w = jnp.asarray

    def _rec_inputs():
        import jax
        import jax.numpy as jnp
        _rk = jax.random.key(seed)
        x = 7.22e-05 + 1 * jax.random.normal(jax.random.fold_in(_rk, 1), (128, 64, 128), jnp.float32)
        _lenS = 64 - jax.random.randint(jax.random.fold_in(_rk, 7), (128,), 0, max(1, 64 // 4) + 1, jnp.int32)
        _lenS2 = 64 - jax.random.randint(jax.random.fold_in(_rk, 8), (128,), 0, max(1, 64 // 4) + 1, jnp.int32)
        _ctx_1024P = jax.random.normal(jax.random.fold_in(_rk, 11), (128, 16, 128), jnp.float32)
        _ctx_1024c = jax.random.dirichlet(jax.random.fold_in(_rk, 511), 0.3 * jnp.ones((16,), jnp.float32), (128, 64))
        _ctx_1024t = jnp.einsum('bsk,bkd->bsd', _ctx_1024c, _ctx_1024P)
        _ctx_1024t = _ctx_1024t * jax.lax.rsqrt(jnp.mean(jnp.square(_ctx_1024t)) + 1e-12) * 0.953939
        ctx_1024 = 4.13588e-05 + 0.999923 * (_ctx_1024t + 0.3 * jax.random.normal(jax.random.fold_in(_rk, 611), (128, 64, 128), jnp.float32))
        return (x, ctx_1024)
    x, ctx_1024 = _rec_inputs()

    def _L0_attn_setup():
        import jax, jax.numpy as jnp
        import numpy as np
        from functools import partial
        LN_EPS = 1000000.0
        FEAT_EPS = 1e-06

        def _layernorm(x, gamma, beta):
            mu = jnp.mean(x, axis=-1, keepdims=True)
            var = jnp.var(x, axis=-1, keepdims=True)
            return gamma * (x - mu) / jnp.sqrt(var + LN_EPS) + beta

        def _phi(x, omega):
            m = omega.shape[0]
            proj = jnp.einsum('bhsd,md->bhsm', x, omega)
            z = proj - 0.5 * jnp.sum(x * x, axis=-1, keepdims=True)
            z = z - jnp.max(z, axis=-1, keepdims=True)
            return jnp.exp(z) / jnp.sqrt(jnp.asarray(m, x.dtype)) + FEAT_EPS

        def _forward(batch, Wq, Wk, Wv, Wo, omega, W1, b1, W2, b2, gamma, beta):
            B, S, D = batch.shape
            M, dh = omega.shape
            H = D // dh
            scale = dh ** (-0.25)

            def heads(W):
                return (batch @ W).reshape(B, S, H, dh).transpose(0, 2, 1, 3)
            q = heads(Wq) * scale
            k = heads(Wk) * scale
            v = heads(Wv)
            qp = _phi(q, omega)
            kp = _phi(k, omega)
            qs = qp.transpose(2, 0, 1, 3)
            ks = kp.transpose(2, 0, 1, 3)
            vs = v.transpose(2, 0, 1, 3)

            def step(carry, qkv):
                S_kv, s_k = carry
                qt, kt, vt = qkv
                S_kv = S_kv + kt[..., :, None] * vt[..., None, :]
                s_k = s_k + kt
                num = jnp.einsum('bhm,bhmd->bhd', qt, S_kv)
                den = jnp.einsum('bhm,bhm->bh', qt, s_k)
                return ((S_kv, s_k), num / (den[..., None] + FEAT_EPS))
            carry0 = (jnp.zeros((B, H, M, dh), batch.dtype), jnp.zeros((B, H, M), batch.dtype))
            _, outs = jax.lax.scan(step, carry0, (qs, ks, vs))
            attn = outs.transpose(1, 0, 2, 3).reshape(B, S, D) @ Wo
            h = _layernorm(batch + attn, gamma, beta)
            out = jnp.maximum(h @ W1 + b1, 0.0) @ W2 + b2
            return out
        key = jax.random.key(seed)
        ks = jax.random.split(key, 8)
        B, S, D, H, dh, M, DFF = (4, 128, 128, 16, 64, 128, 512)
        w = 0.02
        return {'batch': jax.random.normal(ks[0], (B, S, D), jnp.float32), 'Wq': jax.random.normal(ks[1], (D, D), jnp.float32) * w, 'Wk': jax.random.normal(ks[2], (D, D), jnp.float32) * w, 'Wv': jax.random.normal(ks[3], (D, D), jnp.float32) * w, 'Wo': jax.random.normal(ks[4], (D, D), jnp.float32) * w, 'omega': jax.random.normal(ks[5], (M, dh), jnp.float32), 'W1': jax.random.normal(ks[6], (D, DFF), jnp.float32) * w, 'b1': jnp.zeros((DFF,), jnp.float32), 'W2': jax.random.normal(ks[7], (DFF, D), jnp.float32) * w, 'b2': jnp.zeros((D,), jnp.float32), 'gamma': jnp.ones((D,), jnp.float32), 'beta': jnp.zeros((D,), jnp.float32)}
    _L0_attn_all = _L0_attn_setup()
    _L0_attn_in = {k: v for k, v in _L0_attn_all.items() if k in ('Wq', 'Wk', 'Wv', 'Wo', 'omega', 'W1', 'b1', 'W2', 'b2', 'gamma', 'beta')}
    del _L0_attn_all

    def _L0_xattn_setup():
        import jax, jax.numpy as jnp
        import numpy as np
        EMBED_DIM = 128
        HEAD_DIM = 128
        GAMMA = 0.96875
        THETA = 10000.0
        SCALE_BASE = 512.0

        def _dup_interleave(x):
            return jnp.repeat(x, 2, axis=-1)

        def _rotate_half(x):
            x_even = x[..., ::2]
            x_odd = x[..., 1::2]
            return jnp.stack((-x_odd, x_even), axis=-1).reshape(x.shape)

        def _xpos(x, offset=0, inverse_scale=False):
            l = x.shape[-2]
            half = HEAD_DIM // 2
            scale_vec = (jnp.arange(0, HEAD_DIM, 2, dtype=jnp.float32) + 0.4 * HEAD_DIM) / (1.4 * HEAD_DIM)
            pos = jnp.arange(offset, offset + l, dtype=jnp.float32)
            scale = scale_vec[None, :] ** (pos / SCALE_BASE)[:, None]
            freqs = 1.0 / THETA ** (jnp.arange(half, dtype=jnp.float32) / half)
            sin_in = pos[:, None] * freqs[None, :]
            sin, cos = (jnp.sin(sin_in), jnp.cos(sin_in))
            if inverse_scale:
                scale = 1.0 / scale
            return x * _dup_interleave(cos * scale) + _rotate_half(x) * _dup_interleave(sin * scale)

        def _decay_mask(l, gamma):
            idx = jnp.arange(l, dtype=jnp.float32)
            diff = idx[:, None] - idx[None, :]
            return jnp.where(diff >= 0, gamma ** diff, 0.0)
        key = jax.random.key(seed)
        k1, k2, k3, k4, k5, k6 = jax.random.split(key, 6)
        B, L = (4, 256)
        s = 1.0 / np.sqrt(EMBED_DIM)
        return {'q': jax.random.normal(k1, (B, L, EMBED_DIM), dtype=jnp.float32), 'k': jax.random.normal(k2, (B, L, EMBED_DIM), dtype=jnp.float32), 'v': jax.random.normal(k3, (B, L, EMBED_DIM), dtype=jnp.float32), 'Wq': jax.random.normal(k4, (EMBED_DIM, HEAD_DIM), dtype=jnp.float32) * s, 'Wk': jax.random.normal(k5, (EMBED_DIM, HEAD_DIM), dtype=jnp.float32) * s, 'Wv': jax.random.normal(k6, (EMBED_DIM, HEAD_DIM), dtype=jnp.float32) * s}
    _L0_xattn_all = _L0_xattn_setup()
    _L0_xattn_in = {k: v for k, v in _L0_xattn_all.items() if k in ('Wq', 'Wk', 'Wv')}
    del _L0_xattn_all

    def _L0_ffn_setup():
        import jax, jax.numpy as jnp
        import numpy as np
        from jax import lax
        T, B, I, M, O = (32, 64, 128, 128, 128)

        def _xavier(key, shape):
            fan_out, fan_in = shape
            limit = float(np.sqrt(6.0 / (fan_in + fan_out)))
            return jax.random.uniform(key, shape, jnp.float32, -limit, limit)
        key = jax.random.key(seed)
        ks = jax.random.split(key, 9)
        x = jax.random.normal(ks[0], (T, B, I), jnp.float32)
        return {'x': x, 'wf': _xavier(ks[1], (M, I)), 'uf': _xavier(ks[2], (M, M)), 'bf': jnp.zeros((M,), jnp.float32), 'wi': _xavier(ks[3], (M, I)), 'ui': _xavier(ks[4], (M, M)), 'bi': jnp.zeros((M,), jnp.float32), 'wc': _xavier(ks[5], (M, I)), 'uc': _xavier(ks[6], (M, M)), 'bc': jnp.zeros((M,), jnp.float32), 'wo': _xavier(ks[7], (O, I)), 'uo': _xavier(ks[8], (O, M)), 'bo': jnp.zeros((O,), jnp.float32), 'in_c': jnp.zeros((M,), jnp.float32)}
    _L0_ffn_all = _L0_ffn_setup()
    _L0_ffn_in = {k: v for k, v in _L0_ffn_all.items() if k in ('wf', 'uf', 'bf', 'wi', 'ui', 'bi', 'wc', 'uc', 'bc', 'wo', 'uo', 'bo', 'in_c')}
    del _L0_ffn_all
    return {'x': x, 'ctx_1024': ctx_1024, 'L0_attn_Wq': _L0_attn_in['Wq'], 'L0_attn_Wk': _L0_attn_in['Wk'], 'L0_attn_Wv': _L0_attn_in['Wv'], 'L0_attn_Wo': _L0_attn_in['Wo'], 'L0_attn_omega': _L0_attn_in['omega'], 'L0_attn_W1': _L0_attn_in['W1'], 'L0_attn_b1': _L0_attn_in['b1'], 'L0_attn_W2': _L0_attn_in['W2'], 'L0_attn_b2': _L0_attn_in['b2'], 'L0_attn_gamma': _L0_attn_in['gamma'], 'L0_attn_beta': _L0_attn_in['beta'], 'L0_xattn_Wq': _L0_xattn_in['Wq'], 'L0_xattn_Wk': _L0_xattn_in['Wk'], 'L0_xattn_Wv': _L0_xattn_in['Wv'], 'L0_ffn_wf': _L0_ffn_in['wf'], 'L0_ffn_uf': _L0_ffn_in['uf'], 'L0_ffn_bf': _L0_ffn_in['bf'], 'L0_ffn_wi': _L0_ffn_in['wi'], 'L0_ffn_ui': _L0_ffn_in['ui'], 'L0_ffn_bi': _L0_ffn_in['bi'], 'L0_ffn_wc': _L0_ffn_in['wc'], 'L0_ffn_uc': _L0_ffn_in['uc'], 'L0_ffn_bc': _L0_ffn_in['bc'], 'L0_ffn_wo': _L0_ffn_in['wo'], 'L0_ffn_uo': _L0_ffn_in['uo'], 'L0_ffn_bo': _L0_ffn_in['bo'], 'L0_ffn_in_c': _L0_ffn_in['in_c']}

def reference(x, ctx_1024, L0_attn_Wq, L0_attn_Wk, L0_attn_Wv, L0_attn_Wo, L0_attn_omega, L0_attn_W1, L0_attn_b1, L0_attn_W2, L0_attn_b2, L0_attn_gamma, L0_attn_beta, L0_xattn_Wq, L0_xattn_Wk, L0_xattn_Wv, L0_ffn_wf, L0_ffn_uf, L0_ffn_bf, L0_ffn_wi, L0_ffn_ui, L0_ffn_bi, L0_ffn_wc, L0_ffn_uc, L0_ffn_bc, L0_ffn_wo, L0_ffn_uo, L0_ffn_bo, L0_ffn_in_c):
    import jax
    import jax.numpy as jnp

    def _L0_attn_ref(batch, Wq, Wk, Wv, Wo, omega, W1, b1, W2, b2, gamma, beta):
        import jax, jax.numpy as jnp
        import numpy as np
        from functools import partial
        LN_EPS = 1000000.0
        FEAT_EPS = 1e-06

        def _layernorm(x, gamma, beta):
            mu = jnp.mean(x, axis=-1, keepdims=True)
            var = jnp.var(x, axis=-1, keepdims=True)
            return gamma * (x - mu) / jnp.sqrt(var + LN_EPS) + beta

        def _phi(x, omega):
            m = omega.shape[0]
            proj = jnp.einsum('bhsd,md->bhsm', x, omega)
            z = proj - 0.5 * jnp.sum(x * x, axis=-1, keepdims=True)
            z = z - jnp.max(z, axis=-1, keepdims=True)
            return jnp.exp(z) / jnp.sqrt(jnp.asarray(m, x.dtype)) + FEAT_EPS

        def _forward(batch, Wq, Wk, Wv, Wo, omega, W1, b1, W2, b2, gamma, beta):
            B, S, D = batch.shape
            M, dh = omega.shape
            H = D // dh
            scale = dh ** (-0.25)

            def heads(W):
                return (batch @ W).reshape(B, S, H, dh).transpose(0, 2, 1, 3)
            q = heads(Wq) * scale
            k = heads(Wk) * scale
            v = heads(Wv)
            qp = _phi(q, omega)
            kp = _phi(k, omega)
            qs = qp.transpose(2, 0, 1, 3)
            ks = kp.transpose(2, 0, 1, 3)
            vs = v.transpose(2, 0, 1, 3)

            def step(carry, qkv):
                S_kv, s_k = carry
                qt, kt, vt = qkv
                S_kv = S_kv + kt[..., :, None] * vt[..., None, :]
                s_k = s_k + kt
                num = jnp.einsum('bhm,bhmd->bhd', qt, S_kv)
                den = jnp.einsum('bhm,bhm->bh', qt, s_k)
                return ((S_kv, s_k), num / (den[..., None] + FEAT_EPS))
            carry0 = (jnp.zeros((B, H, M, dh), batch.dtype), jnp.zeros((B, H, M), batch.dtype))
            _, outs = jax.lax.scan(step, carry0, (qs, ks, vs))
            attn = outs.transpose(1, 0, 2, 3).reshape(B, S, D) @ Wo
            h = _layernorm(batch + attn, gamma, beta)
            out = jnp.maximum(h @ W1 + b1, 0.0) @ W2 + b2
            return out
        return _forward(batch, Wq, Wk, Wv, Wo, omega, W1, b1, W2, b2, gamma, beta)

    def _L0_xattn_ref(q, k, v, Wq, Wk, Wv):
        import jax, jax.numpy as jnp
        import numpy as np
        EMBED_DIM = 128
        HEAD_DIM = 128
        GAMMA = 0.96875
        THETA = 10000.0
        SCALE_BASE = 512.0

        def _dup_interleave(x):
            return jnp.repeat(x, 2, axis=-1)

        def _rotate_half(x):
            x_even = x[..., ::2]
            x_odd = x[..., 1::2]
            return jnp.stack((-x_odd, x_even), axis=-1).reshape(x.shape)

        def _xpos(x, offset=0, inverse_scale=False):
            l = x.shape[-2]
            half = HEAD_DIM // 2
            scale_vec = (jnp.arange(0, HEAD_DIM, 2, dtype=jnp.float32) + 0.4 * HEAD_DIM) / (1.4 * HEAD_DIM)
            pos = jnp.arange(offset, offset + l, dtype=jnp.float32)
            scale = scale_vec[None, :] ** (pos / SCALE_BASE)[:, None]
            freqs = 1.0 / THETA ** (jnp.arange(half, dtype=jnp.float32) / half)
            sin_in = pos[:, None] * freqs[None, :]
            sin, cos = (jnp.sin(sin_in), jnp.cos(sin_in))
            if inverse_scale:
                scale = 1.0 / scale
            return x * _dup_interleave(cos * scale) + _rotate_half(x) * _dup_interleave(sin * scale)

        def _decay_mask(l, gamma):
            idx = jnp.arange(l, dtype=jnp.float32)
            diff = idx[:, None] - idx[None, :]
            return jnp.where(diff >= 0, gamma ** diff, 0.0)
        qh = _xpos(q @ Wq, offset=0, inverse_scale=False)
        kh = _xpos(k @ Wk, offset=0, inverse_scale=True)
        vh = v @ Wv
        L = qh.shape[-2]
        mask = _decay_mask(L, GAMMA)
        scores = jnp.einsum('bld,bmd->blm', qh, kh) * mask[None, :, :]
        return scores @ vh

    def _L0_ffn_ref(x, wf, uf, bf, wi, ui, bi, wc, uc, bc, wo, uo, bo, in_c):
        import jax, jax.numpy as jnp
        import numpy as np
        from jax import lax
        T, B, I, M, O = (32, 64, 128, 128, 128)

        def _xavier(key, shape):
            fan_out, fan_in = shape
            limit = float(np.sqrt(6.0 / (fan_in + fan_out)))
            return jax.random.uniform(key, shape, jnp.float32, -limit, limit)
        batch = x.shape[1]
        c0 = jnp.broadcast_to(in_c, (batch, in_c.shape[0]))

        def step(c, xt):
            ft = jax.nn.sigmoid(xt @ wf.T + c @ uf.T + bf)
            it = jax.nn.sigmoid(xt @ wi.T + c @ ui.T + bi)
            gt = jnp.tanh(xt @ wc.T + c @ uc.T + bc)
            c = ft * c + it * gt
            return (c, None)
        c_final, _ = lax.scan(step, c0, x)
        h = jnp.tanh(jnp.einsum('tbi,oi->tbo', x, wo) + c_final @ uo.T + bo)
        return h
    x = _layernorm(x + _L0_attn_ref(x, L0_attn_Wq, L0_attn_Wk, L0_attn_Wv, L0_attn_Wo, L0_attn_omega, L0_attn_W1, L0_attn_b1, L0_attn_W2, L0_attn_b2, L0_attn_gamma, L0_attn_beta), axis=-1)
    x = _layernorm(x + _L0_xattn_ref(x, ctx_1024, ctx_1024, L0_xattn_Wq, L0_xattn_Wk, L0_xattn_Wv), axis=-1)
    x = _layernorm(x + _L0_ffn_ref(x, L0_ffn_wf, L0_ffn_uf, L0_ffn_bf, L0_ffn_wi, L0_ffn_ui, L0_ffn_bi, L0_ffn_wc, L0_ffn_uc, L0_ffn_bc, L0_ffn_wo, L0_ffn_uo, L0_ffn_bo, L0_ffn_in_c), axis=-1)
    return x

_drawn_inputs = setup_inputs


def setup_inputs(seed=0):
    import zlib

    import numpy as np

    out = dict(_drawn_inputs(seed))
    spreads = {'L0_attn_b1': (0.0, 0.1),
     'L0_attn_b2': (0.0, 0.1),
     'L0_attn_gamma': (1.0, 0.6),
     'L0_attn_beta': (0.0, 0.8),
     'L0_ffn_bf': (0.0, 0.696),
     'L0_ffn_bi': (0.0, 0.676),
     'L0_ffn_bc': (0.0, 0.1),
     'L0_ffn_bo': (0.0, 0.1),
     'L0_ffn_in_c': (0.0, 2.0)}
    factors = {'L0_attn_Wq': 64.0,
     'L0_attn_Wk': 64.0,
     'L0_attn_Wv': 64.0,
     'L0_attn_Wo': 64.0,
     'L0_attn_omega': 64.0,
     'L0_attn_W1': 7.869}
    for name, (base, spread) in spreads.items():
        noise = np.random.default_rng([zlib.crc32(name.encode()), seed]).standard_normal(out[name].shape)
        drawn = base * np.exp(spread * noise) if base else spread * noise
        out[name] = jnp.asarray(drawn.astype(out[name].dtype))
    for name, factor in factors.items():
        out[name] = (out[name] * factor).astype(out[name].dtype)
    return out
```

```python
from contextlib import ExitStack

import numpy as np
import concourse.bass as bass
from concourse import mybir

F32 = mybir.dt.float32
BF16 = mybir.dt.bfloat16
ALU = mybir.AluOpType
ACT = mybir.ActivationFunctionType
AX = mybir.AxisListType

P = 128
SEQS, SEQ, D = 128, 64, 128
TOKENS = SEQS * SEQ
T = 2
BT = T * P
NB = TOKENS // BT
STEPS = BT // SEQ
HEADS, DH, M = 2, 64, 128
FC = 4
VW = D + 1
GT = 4
NG = TOKENS // (GT * P)

FEAT_EPS = 1e-6
LN_EPS = 1e-5
ATTN_LN_EPS = 1e6
GAMMA, THETA, SCALE_BASE = 0.96875, 10000.0, 512.0

W_COLS = [("aq_T", D), ("ak_T", D), ("av_T", D), ("ao", D), ("omega_T", M), ("aq", D), ("ak", D),
          ("w1", FC * P), ("w2", FC * P), ("b1", FC), ("gamma", 1), ("beta", 1), ("b2", D),
          ("rq", D), ("rk", D), ("rv", D), ("wf", D), ("wi", D), ("wc", D),
          ("uf", D), ("ui", D), ("uc", D), ("wo", D), ("uo", D), ("c0", 1)]
C_COLS = [("ident", P), ("causal", P), ("decay", P), ("q_cos", SEQ), ("q_sin", SEQ),
          ("k_cos", SEQ), ("k_sin", SEQ), ("part", 3)]


def offsets(cols):
    at, where = 0, {}
    for name, n in cols:
        where[name] = (at, at + n)
        at += n
    return where, at


def program(nc, x_rows, x_cols, ctx_cols, weights, bias_rows, consts, out):
    wat, wn = offsets(W_COLS)
    cat, cn = offsets(C_COLS)
    LAST = NB + 3
    LOOP0 = 4

    def live(b):
        return not isinstance(b, int) or 0 <= b < NB

    def nth(b, per, k):
        return b * per + k

    with ExitStack() as ctx:
        def sb(name, shape, dt=F32):
            return ctx.enter_context(nc.sbuf_tensor(name, shape, dt))

        def sem(name):
            return ctx.enter_context(nc.semaphore(name))

        wts = sb("wts", [P, wn])
        con = sb("con", [P, cn])
        bias_in = sb("bias_in", [3, 4 * D])
        bias_rest = sb("bias_rest", [3, 4 * D])
        bias_sum = sb("bias_sum", [3, 4 * D])
        bias_piece = sb("bias_piece", [3, 3, 4 * D], BF16)
        bias_parts = sb("bias_parts", [3, 4 * D], BF16)
        ones3 = sb("ones3", [3, P], BF16)
        front_w = sb("front_w", [P, 8 * P])
        rq_rot = sb("rq_rot", [P, D])
        rk_rot = sb("rk_rot", [P, D])
        gate_w = sb("gate_w", [P, 3, D])
        gate_u = sb("gate_u", [P, 3, D])
        out_u = sb("out_u", [P, D])
        ln_eps = sb("ln_eps", [P, 2, 4])
        minus_half = sb("minus_half", [P, 4])

        def w(name):
            return wts[:, wat[name][0]:wat[name][1]]

        def c(name):
            return con[:, cat[name][0]:cat[name][1]]

        ident = c("ident")

        xT = sb("xT", [P, BT])
        x_attn = sb("x_attn", [P, T, D])
        x_mlp = sb("x_mlp", [P, T, D])
        x_mlp_b = sb("x_mlp_b", [P, T, D])
        ctxT = sb("ctxT", [P, BT])
        qk_sq = sb("qk_sq", [P, T, 2 * D])
        z_top = sb("z_top", [P, T, 4])
        sq_sum = sb("sq_sum", [P, T, 4])
        z_max = sb("z_max", [P, T, 4])
        z_bias = sb("z_bias", [P, T, 4])
        feat = sb("feat", [P, T, 4 * M])
        featT = sb("featT", [P, T, 4 * P])
        values = sb("values", [P, T, HEADS, VW])
        attn_w = sb("attn_w", [P, T, HEADS * P])
        den = sb("den", [P, T, HEADS])
        rden = sb("rden", [P, T, HEADS])
        u = sb("u", [P, T, D])
        u_n = sb("u_n", [P, T, D])
        hT = sb("hT", [P, BT])
        hidden = sb("hidden", [P, FC, BT])
        s1 = sb("s1", [P, T, D])
        x1 = sb("x1", [P, T, D])
        x1T = sb("x1T", [P, BT])
        q_c = sb("q_c", [P, BT])
        q_s = sb("q_s", [P, BT])
        qT = sb("qT", [P, BT])
        k_c = sb("k_c", [P, BT])
        k_s = sb("k_s", [P, BT])
        kT = sb("kT", [P, BT])
        rv = sb("rv_tok", [P, T, D])
        ret_w = sb("ret_w", [P, T, P])
        s2 = sb("s2", [P, T, D])
        x2 = sb("x2", [P, T, D])
        x2T = sb("x2T", [P, BT])
        st = [sb(f"st{n}", [P, T, 6]) for n in range(3)]
        mv = [sb(f"mv{n}", [P, T, 2]) for n in range(3)]
        ve = [sb(f"ve{n}", [P, T]) for n in range(3)]
        rstd = [sb(f"rstd{n}", [P, T]) for n in range(3)]
        wait_slot = sb("wait_slot", [P, 1])
        state = sb("state", [P, SEQ])
        gates = sb("gates", [P, 3, SEQ])
        keep = sb("keep", [P, SEQ])
        gain = sb("gain", [P, SEQ])
        x2_all = sb("x2_all", [P, TOKENS])
        zo_all = sb("zo_all", [P, TOKENS])
        state2 = sb("state2", [P, 2, SEQ])
        add_row = sb("add_row", [P, D])
        e_in = sb("e_in", [P, 2, GT * D])
        e_h = sb("e_h", [P, 2, GT * D])
        e_s = sb("e_s", [P, 2, GT * D])
        e_o = sb("e_o", [P, 2, GT * D])
        e_st = sb("e_st", [P, 2, GT, 6])
        e_mv = sb("e_mv", [P, 2, GT, 2])
        e_ve = sb("e_ve", [P, 2, GT])
        e_rs = sb("e_rs", [P, 2, GT])

        bank = [ctx.enter_context(nc.psum_tensor(f"bank{n}", [P, 512], F32)) for n in range(8)]
        GATE = [bank[0], bank[1]]
        Z = [bank[2], bank[4]]
        VQ = [bank[3], bank[5]]
        ZO, NORM_T, Q, HID, FEAT_T = bank[7], bank[6], bank[3], [bank[6], bank[7]], [bank[2], bank[4]]
        RSC, Y, ASC, ROUT, K, V = bank[5], bank[3], bank[6], bank[7], bank[2], bank[4]
        NUM, X1_T, X2_T = [bank[5], bank[6]], bank[3], bank[7]

        w_in, xT_in, xa_in, xb_in, ctx_in = (sem(n) for n in ("w_in", "xT_in", "xa_in", "xb_in", "ctx_in"))
        prep_mm, prep_dve, prep_pool, prep_chain = (sem(n) for n in ("prep_mm", "prep_dve", "prep_pool", "prep_chain"))
        (proj_mm, gatex_mm, zo_mm, step_mm, norm_T, q_mm, hid_mm, feat_T, rsc_mm, y_mm, asc_mm,
         rout_mm, k_mm, v_mm, num_mm, x1_T, x2_T) = (sem(n) for n in (
             "proj_mm", "gatex_mm", "zo_mm", "step_mm", "norm_T", "q_mm", "hid_mm", "feat_T",
             "rsc_mm", "y_mm", "asc_mm", "rout_mm", "k_mm", "v_mm", "num_mm", "x1_T", "x2_T"))
        sq_a, val_a, exp_a, hT_a, hid_a, featT_a, v_a, x1T_a, x2T_a, tanh_a = (sem(n) for n in (
            "sq_a", "val_a", "exp_a", "hT_a", "hid_a", "featT_a", "v_a", "x1T_a", "x2T_a", "tanh_a"))
        (top_v, max_v, bias_v, zo_v, parts_v, state_v, un_v, qmul_v, rw_v, s1_v, aw_v, s2_v, x1_v,
         kmul_v, den_v, rden_v, u0_v, u_v, x2_v) = (sem(n) for n in (
             "top_v", "max_v", "bias_v", "zo_v", "parts_v", "state_v", "un_v", "qmul_v", "rw_v",
             "s1_v", "aw_v", "s2_v", "x1_v", "kmul_v", "den_v", "rden_v", "u0_v", "u_v", "x2_v"))
        st_v = [sem(f"st{n}_v") for n in range(3)]
        mv_v = [sem(f"mv{n}_v") for n in range(3)]
        ve_p = [sem(f"ve{n}_p") for n in range(3)]
        rs_p = [sem(f"rs{n}_p") for n in range(3)]
        q_p, k_p, xb_p, keep_p = (sem(n) for n in ("q_p", "k_p", "xb_p", "keep_p"))
        (f_st2, f_add_mm, f_add, f_in, f_tanh, f_s, f_st, f_mv, f_ve, f_rs, f_o, f_out) = (sem(n) for n in (
            "f_st2", "f_add_mm", "f_add", "f_in", "f_tanh", "f_s", "f_st", "f_mv", "f_ve", "f_rs",
            "f_o", "f_out"))
        f_out1 = sem("f_out1")
        stored = [f_out, f_out1]

        block = ctx.enter_context(nc.Block())

        @block.sync
        def _(sp):
            sp.dma_start(wts[:], weights).then_inc(w_in, 16)
            sp.dma_start(con[:], consts).then_inc(w_in, 16)
            sp.dma_start(bias_in[:], bias_rows).then_inc(w_in, 16)

            def step(j):
                if live(j):
                    b = j
                    if live(b - 1):
                        sp.wait_ge(proj_mm, nth(b - 1, T, T))
                    sp.dma_start(xT[:], x_cols[bass.ds(b, 1), :, :].rearrange("o p n -> (o p) n")
                                 ).then_inc(xT_in, 16)
                if live(j - 1):
                    b = j - 1
                    if live(b - 1):
                        sp.wait_ge(u_v, nth(b - 1, T, T))
                    sp.dma_start(x_attn[:].rearrange("p t d -> p (t d)"),
                                 x_rows[bass.ds(b, 1), :, :].rearrange("o p n -> (o p) n")
                                 ).then_inc(xa_in, 16)
                if live(j - 2):
                    b = j - 2
                    if live(b - 1):
                        sp.wait_ge(xb_p, nth(b - 1, 1, 1))
                    sp.dma_start(x_mlp[:].rearrange("p t d -> p (t d)"),
                                 x_rows[bass.ds(b, 1), :, :].rearrange("o p n -> (o p) n")
                                 ).then_inc(xb_in, 16)
                    if live(b - 1):
                        sp.wait_ge(v_mm, nth(b - 1, 1, 1))
                    sp.dma_start(ctxT[:], ctx_cols[bass.ds(b, 1), :, :].rearrange("o p n -> (o p) n")
                                 ).then_inc(ctx_in, 16)

            for j in range(LOOP0):
                step(j)
            with sp.Fori(LOOP0, NB) as j:
                step(j)
            for j in range(NB, NB + 2):
                step(j)

            def store(g, odd):
                sp.wait_ge(f_o, g + 1)
                sp.dma_start(out[bass.ds(g, 1), :, :].rearrange("o p n -> (o p) n"),
                             e_o[:, odd, :]).then_inc(stored[odd], 16)

            with sp.Fori(0, NG - 1, 2) as g:
                store(g, 0)
                store(g + 1, 1)
            for odd in range(2):
                sp.wait_ge(stored[odd], 16 * (NG // 2))

        @block.tensor
        def _(pe):
            pe.wait_ge(w_in, 48)
            for h in range(HEADS):
                r = slice(DH * h, DH * h + DH)
                pe.matmul(bank[2 + h][:, 0:P], w("aq_T")[r, :], w("omega_T")[r, :], start=True, stop=True)
                pe.matmul(bank[2 + h][:, P:2 * P], w("ak_T")[r, :], w("omega_T")[r, :], start=True, stop=True)
                pe.matmul(bank[2 + h][:, 2 * P:3 * P], w("av_T")[r, :], w("ao")[r, :],
                          start=True, stop=True).then_inc(prep_mm, 1)
            pe.wait_ge(prep_dve, 1)
            pe.wait_ge(prep_pool, 1)

            def front(b, t):
                if t == 0:
                    pe.wait_ge(xT_in, nth(b, 16, 16))
                if live(b - 2) and t == 0:
                    pe.wait_ge(kmul_v, nth(b - 2, 1, 1))
                if live(b - 2) and t == 0:
                    pe.wait_ge(x1T_a, nth(b - 2, 1, 1))
                if live(b - 2) and t == 1:
                    pe.wait_ge(v_a, nth(b - 2, 1, 1))
                if live(b - 1) and t == 1:
                    pe.wait_ge(u_v, nth(b - 1, T, 1))
                tile = xT[:, t * P:(t + 1) * P]
                pe.matmul(Z[t][:], tile, front_w[:, 0:512], start=True, stop=True)
                pe.matmul(VQ[t][:], tile, front_w[:, 512:1024], start=True, stop=True).then_inc(proj_mm, 1)

            def gates_x(b):
                pe.wait_ge(x2T_a, nth(b, 1, 1))
                if live(b - 1):
                    pe.wait_ge(tanh_a, nth(b - 1, STEPS, STEPS))
                for t in range(T):
                    for g in range(3):
                        pe.matmul(GATE[t][:, g * P:(g + 1) * P], bias_parts[:, g * D:(g + 1) * D], ones3[:],
                                  start=(g == 0), stop=False, skip_group_check=True)
                    for g in range(3):
                        mm = pe.matmul(GATE[t][:, g * P:(g + 1) * P], gate_w[:, g, :],
                                       x2T[:, t * P:(t + 1) * P], start=False, stop=False,
                                       skip_group_check=True)
                for t in range(T):
                    mm = pe.matmul(ZO[:, t * P:(t + 1) * P], x2T[:, t * P:(t + 1) * P], w("wo"),
                                   start=True, stop=True)
                mm.then_inc(zo_mm, 1)

            def step(b, k):
                pe.wait_ge(state_v, nth(b, STEPS, k + 1))
                t, half = k // 2, k % 2
                for g in range(3):
                    at = g * P + half * SEQ
                    mm = pe.matmul(GATE[t][:, at:at + SEQ], gate_u[:, g, :], state[:],
                                   start=False, stop=True, skip_group_check=True)
                mm.then_inc(step_mm, 1)

            def turn(dst, src, done):
                for t in range(T):
                    mm = pe.transpose(dst[:, t * P:(t + 1) * P], src[:, t, :], ident)
                mm.then_inc(done, 1)

            def body(i):
                if live(i):
                    front(i, 0)
                if live(i - 3):
                    gates_x(i - 3)
                    step(i - 3, 0)
                if live(i):
                    front(i, 1)
                if live(i - 1):
                    pe.wait_ge(un_v, nth(i - 1, 1, 1))
                    turn(NORM_T, u_n, norm_T)
                if live(i - 2):
                    pe.wait_ge(x1T_a, nth(i - 2, 1, 1))
                    if live(i):
                        pe.wait_ge(sq_a, nth(i, T, 1))
                        pe.wait_ge(val_a, nth(i, T, 1))
                    pe.matmul(Q[:, 0:BT], w("rq"), x1T[:], start=True, stop=True)
                    pe.matmul(Q[:, BT:2 * BT], rq_rot[:], x1T[:], start=True, stop=True).then_inc(q_mm, 1)
                if live(i - 1):
                    pe.wait_ge(hT_a, nth(i - 1, 1, 1))
                    if live(i - 3):
                        pe.wait_ge(zo_v, nth(i - 3, 1, 1))
                    for f in range(FC):
                        mm = pe.matmul(HID[f // 2][:, (f % 2) * BT:(f % 2 + 1) * BT],
                                       w("w1")[:, f * P:(f + 1) * P], hT[:], start=True, stop=True)
                        if f % 2 == 1:
                            mm.then_inc(hid_mm, 1)
                if live(i - 3):
                    step(i - 3, 1)
                if live(i):
                    for t in range(T):
                        pe.wait_ge(exp_a, nth(i, T, t + 1))
                        for j in range(4):
                            mm = pe.transpose(FEAT_T[t][:, j * P:(j + 1) * P],
                                              feat[:, t, j * M:(j + 1) * M], ident)
                        mm.then_inc(feat_T, 1)
                if live(i - 2):
                    pe.wait_ge(q_p, nth(i - 2, 1, 1))
                    pe.wait_ge(k_p, nth(i - 2, 1, 1))
                    if live(i):
                        pe.wait_ge(sq_a, nth(i, T, 2))
                        pe.wait_ge(val_a, nth(i, T, 2))
                    for t in range(T):
                        r = slice(t * P, (t + 1) * P)
                        mm = pe.matmul(RSC[:, r], kT[:, r], qT[:, r], start=True, stop=True)
                    mm.then_inc(rsc_mm, 1)
                if live(i - 1):
                    pe.wait_ge(hid_a, nth(i - 1, FC, FC))
                    for t in range(T):
                        for f in range(FC):
                            mm = pe.matmul(Y[:, t * P:(t + 1) * P], hidden[:, f, t * P:(t + 1) * P],
                                           w("w2")[:, f * P:(f + 1) * P], start=(f == 0), stop=(f == FC - 1))
                    mm.then_inc(y_mm, 1)
                if live(i):
                    pe.wait_ge(featT_a, nth(i, T, T))
                    for t in range(T):
                        for h in range(HEADS):
                            at = (t * HEADS + h) * P
                            mm = pe.matmul(ASC[:, at:at + P], featT[:, t, (HEADS + h) * P:(HEADS + h + 1) * P],
                                           featT[:, t, h * P:(h + 1) * P], start=True, stop=True)
                    mm.then_inc(asc_mm, 1)
                if live(i - 3):
                    step(i - 3, 2)
                if live(i - 2):
                    pe.wait_ge(rw_v, nth(i - 2, 1, 1))
                    pe.wait_ge(v_a, nth(i - 2, 1, 1))
                    for t in range(T):
                        mm = pe.matmul(ROUT[:, t * P:(t + 1) * P], ret_w[:, t, :], rv[:, t, :],
                                       start=True, stop=True)
                    mm.then_inc(rout_mm, 1)
                if live(i - 1):
                    pe.wait_ge(ctx_in, nth(i - 1, 16, 16))
                    pe.matmul(K[:, 0:BT], w("rk"), ctxT[:], start=True, stop=True)
                    pe.matmul(K[:, BT:2 * BT], rk_rot[:], ctxT[:], start=True, stop=True).then_inc(k_mm, 1)
                    for t in range(T):
                        mm = pe.matmul(V[:, t * P:(t + 1) * P], ctxT[:, t * P:(t + 1) * P], w("rv"),
                                       start=True, stop=True)
                    mm.then_inc(v_mm, 1)
                if live(i):
                    pe.wait_ge(aw_v, nth(i, 1, 1))
                    pe.wait_ge(val_a, nth(i, T, T))
                    for t in range(T):
                        for h in range(HEADS):
                            mm = pe.matmul(NUM[t][:, h * VW:(h + 1) * VW], attn_w[:, t, h * P:(h + 1) * P],
                                           values[:, t, h, :], start=True, stop=True)
                        mm.then_inc(num_mm, 1)
                if live(i - 1):
                    pe.wait_ge(x1_v, nth(i - 1, 1, 1))
                    turn(X1_T, x1, x1_T)
                if live(i - 3):
                    step(i - 3, 3)
                if live(i - 2):
                    pe.wait_ge(x2_v, nth(i - 2, 1, 1))
                    turn(X2_T, x2, x2_T)

            for i in range(LOOP0):
                body(i)
            with pe.Fori(LOOP0, NB) as i:
                body(i)
            for i in range(NB, LAST):
                body(i)

            pe.wait_ge(f_st2, 2)
            pe.matmul(bank[2][:, 0:D], ones3[:], bias_parts[:, 3 * D:4 * D], start=True, stop=False)
            pe.matmul(bank[2][:, 0:D], state2[:].rearrange("p a b -> p (a b)"), out_u[:],
                      start=False, stop=True).then_inc(f_add_mm, 1)

        @block.scalar
        def _(act):
            act.wait_ge(w_in, 48)
            act.wait_ge(prep_dve, 1)

            def squares(b, t):
                act.wait_ge(proj_mm, nth(b, T, t + 1))
                act.activation(qk_sq[:, t, :], VQ[t][:, 2 * P:4 * P], ACT.Square).then_inc(sq_a, 1)
                if live(b - 1):
                    act.wait_ge(num_mm, nth(b - 1, T, t + 1))
                act.activation(values[:, t, :, 0:D], VQ[t][:, 0:2 * P].rearrange("p (h d) -> p h d", h=HEADS),
                               ACT.Copy).then_inc(val_a, 1)

            def features(b, t):
                act.wait_ge(bias_v, nth(b, T, t + 1))
                for j in range(4):
                    ins = act.activation(feat[:, t, j * M:(j + 1) * M], Z[t][:, j * P:(j + 1) * P], ACT.Exp,
                                         bias=z_bias[:, t, j:j + 1])
                ins.then_inc(exp_a, 1)

            def tanh(b, k):
                act.wait_ge(step_mm, nth(b, STEPS, k + 1))
                view = GATE[k // 2][:, 0:3 * P].rearrange("p (g n) -> p g n", g=3)
                act.activation(gates[:], view[:, :, (k % 2) * SEQ:(k % 2 + 1) * SEQ], ACT.Tanh).then_inc(tanh_a, 1)

            def body(i):
                if live(i):
                    squares(i, 0)
                    features(i, 0)
                if live(i - 3):
                    tanh(i - 3, 0)
                if live(i):
                    squares(i, 1)
                if live(i - 1):
                    act.wait_ge(norm_T, nth(i - 1, 1, 1))
                    act.activation(hT[:], NORM_T[:, 0:BT], ACT.Identity, bias=w("beta"),
                                   scale=w("gamma")).then_inc(hT_a, 1)
                if live(i):
                    features(i, 1)
                if live(i - 1):
                    for f in range(FC):
                        if f % 2 == 0:
                            act.wait_ge(hid_mm, nth(i - 1, 2, f // 2 + 1))
                        act.activation(hidden[:, f, :], HID[f // 2][:, (f % 2) * BT:(f % 2 + 1) * BT], ACT.Relu,
                                       bias=w("b1")[:, f:f + 1]).then_inc(hid_a, 1)
                if live(i - 3):
                    tanh(i - 3, 1)
                if live(i):
                    for t in range(T):
                        act.wait_ge(feat_T, nth(i, T, t + 1))
                        act.activation(featT[:, t, :], FEAT_T[t][:], ACT.Copy, bias=FEAT_EPS,
                                       scale=float(M) ** -0.5).then_inc(featT_a, 1)
                if live(i - 3):
                    tanh(i - 3, 2)
                if live(i - 1):
                    act.wait_ge(v_mm, nth(i - 1, 1, 1))
                    act.activation(rv[:].rearrange("p t d -> p (t d)"), V[:, 0:BT], ACT.Copy).then_inc(v_a, 1)
                    act.wait_ge(x1_T, nth(i - 1, 1, 1))
                    act.activation(x1T[:], X1_T[:, 0:BT], ACT.Copy).then_inc(x1T_a, 1)
                if live(i - 3):
                    tanh(i - 3, 3)
                if live(i - 2):
                    act.wait_ge(x2_T, nth(i - 2, 1, 1))
                    act.activation(x2T[:], X2_T[:, 0:BT], ACT.Copy).then_inc(x2T_a, 1)

            for i in range(LOOP0):
                body(i)
            with act.Fori(LOOP0, NB) as i:
                body(i)
            for i in range(NB, LAST):
                body(i)

            def last(g, odd, first):
                act.wait_ge(f_in, g + 1)
                if not first:
                    act.wait_ge(f_s, g - 1)
                act.activation(e_h[:, odd, :], e_in[:, odd, :], ACT.Tanh).then_inc(f_tanh, 1)

            last(0, 0, True)
            last(1, 1, True)
            with act.Fori(2, NG - 1, 2) as g:
                last(g, 0, False)
                last(g + 1, 1, False)

        @block.vector
        def _(dve):
            for t in range(T):
                nc.vector.memset(values[:, t, :, D:VW], 1.0)
            dve.memset(ones3[:], 1.0)
            dve.memset(minus_half[:], -0.5)
            dve.memset(ln_eps[:, 0, :], ATTN_LN_EPS)
            dve.memset(ln_eps[:, 1, :], LN_EPS)
            dve.wait_ge(w_in, 48)
            for src, dst in (("rq", rq_rot), ("rk", rk_rot)):
                s = w(src).rearrange("p (n two) -> p n two", two=2)
                d = dst[:].rearrange("p (n two) -> p n two", two=2)
                dve.tensor_scalar(d[:, :, 0], s[:, :, 1], -1.0, None, ALU.mult)
                dve.tensor_copy(d[:, :, 1], s[:, :, 0])
            dve.tensor_copy(bias_piece[:, 0, :], bias_in[:]).then_inc(prep_chain, 1)
            dve.wait_ge(prep_chain, 1)
            dve.tensor_tensor(bias_rest[:], bias_in[:], bias_piece[:, 0, :], ALU.subtract).then_inc(prep_chain, 1)
            dve.wait_ge(prep_chain, 2)
            dve.tensor_copy(bias_piece[:, 1, :], bias_rest[:]).then_inc(prep_chain, 1)
            dve.wait_ge(prep_chain, 3)
            dve.tensor_tensor(bias_rest[:], bias_rest[:], bias_piece[:, 1, :], ALU.subtract).then_inc(prep_chain, 1)
            dve.wait_ge(prep_chain, 4)
            dve.tensor_copy(bias_piece[:, 2, :], bias_rest[:]).then_inc(prep_chain, 1)
            dve.wait_ge(prep_chain, 5)
            pick = c("part")[0:3, :]
            dve.tensor_scalar(bias_sum[:], bias_piece[:, 0, :], pick[:, 0:1], None, ALU.mult).then_inc(prep_chain, 1)
            dve.wait_ge(prep_chain, 6)
            dve.scalar_tensor_tensor(bias_sum[:], bias_piece[:, 1, :], pick[:, 1:2], bias_sum[:], ALU.mult,
                                     ALU.add).then_inc(prep_chain, 1)
            dve.wait_ge(prep_chain, 7)
            dve.scalar_tensor_tensor(bias_sum[:], bias_piece[:, 2, :], pick[:, 2:3], bias_sum[:], ALU.mult,
                                     ALU.add).then_inc(prep_chain, 1)
            dve.wait_ge(prep_chain, 8)
            dve.tensor_scalar(bias_parts[:, 0:2 * D], bias_sum[:, 0:2 * D], 0.5, None, ALU.mult)
            dve.tensor_copy(bias_parts[:, 2 * D:4 * D], bias_sum[:, 2 * D:4 * D])
            dve.memset(state[:], 2.0).then_inc(prep_chain, 1)
            dve.wait_ge(prep_chain, 9)
            dve.tensor_scalar(state[:], state[:], w("c0"), None, ALU.mult).then_inc(state_v, 1)
            dve.wait_ge(prep_mm, HEADS)
            for h in range(HEADS):
                r = slice(h * P, (h + 1) * P)
                dve.tensor_scalar(front_w[:, 0:2 * P][:, r], bank[2 + h][:, 0:P], float(DH) ** -0.25, None, ALU.mult)
                dve.tensor_scalar(front_w[:, 2 * P:4 * P][:, r], bank[2 + h][:, P:2 * P], float(DH) ** -0.25,
                                  None, ALU.mult)
                dve.tensor_copy(front_w[:, 4 * P:6 * P][:, r], bank[2 + h][:, 2 * P:3 * P])
            dve.tensor_copy(front_w[:, 6 * P:7 * P], w("aq"))
            dve.tensor_copy(front_w[:, 7 * P:8 * P], w("ak")).then_inc(prep_dve, 1)
            dve.wait_ge(prep_pool, 1)

            def z_shift(b, t):
                dve.wait_ge(proj_mm, nth(b, T, t + 1))
                dve.tensor_reduce(z_top[:, t, :], Z[t][:].rearrange("p (j m) -> p j m", j=4), AX.X, ALU.max)
                dve.wait_ge(sq_a, nth(b, T, t + 1))
                dve.tensor_reduce(sq_sum[:, t, :], qk_sq[:, t, :].rearrange("p (j d) -> p j d", j=4), AX.X,
                                  ALU.add).then_inc(top_v, 1)
                half_scale2 = -0.5 * float(DH) ** -0.5
                dve.wait_ge(top_v, nth(b, T, t + 1))
                dve.scalar_tensor_tensor(z_max[:, t, :], sq_sum[:, t, :], half_scale2, z_top[:, t, :],
                                         ALU.mult, ALU.add).then_inc(max_v, 1)
                dve.wait_ge(max_v, nth(b, T, t + 1))
                dve.scalar_tensor_tensor(z_bias[:, t, :], sq_sum[:, t, :], half_scale2, z_max[:, t, :],
                                         ALU.mult, ALU.subtract).then_inc(bias_v, 1)

            def cell(b, k):
                dve.wait_ge(tanh_a, nth(b, STEPS, k + 1))
                dve.scalar_tensor_tensor(keep[:], gates[:, 0, :], 1.0, state[:], ALU.add, ALU.mult)
                dve.scalar_tensor_tensor(gain[:], gates[:, 1, :], 1.0, gates[:, 2, :], ALU.add,
                                         ALU.mult).then_inc(parts_v, 1)
                dve.wait_ge(parts_v, nth(b, STEPS, k + 1))
                dve.scalar_tensor_tensor(state[:], keep[:], 0.5, gain[:], ALU.mult, ALU.add).then_inc(state_v, 1)

            def stats(n, src, b):
                for t in range(T):
                    ins = dve.bn_stats(st[n][:, t, :], src[:, t, :])
                ins.then_inc(st_v[n], 1)
                dve.wait_ge(st_v[n], nth(b, 1, 1))
                dve.memset(wait_slot[:], 0.0)
                for t in range(T):
                    ins = dve.bn_aggr(mv[n][:, t, :], st[n][:, t, :])
                ins.then_inc(mv_v[n], 1)

            def normalise(n, dst, src, b, done):
                dve.wait_ge(rs_p[n], nth(b, 1, 1))
                for t in range(T):
                    ins = dve.tensor_scalar(dst[:, t, :], src[:, t, :], mv[n][:, t, 0:1], rstd[n][:, t:t + 1],
                                            ALU.subtract, ALU.mult)
                ins.then_inc(done, 1)

            def turned(table):
                return c(table).unsqueeze(1).broadcast_to([P, STEPS, SEQ])

            def body(i):
                if live(i):
                    z_shift(i, 0)
                if live(i - 1):
                    normalise(0, u_n, u, i - 1, un_v)
                if live(i - 3):
                    dve.wait_ge(zo_mm, nth(i - 3, 1, 1))
                    dve.tensor_copy(zo_all[:, bass.ds((i - 3) * BT, BT)], ZO[:, 0:BT]).then_inc(zo_v, 1)
                    cell(i - 3, 0)
                if live(i):
                    z_shift(i, 1)
                if live(i - 2):
                    dve.wait_ge(q_mm, nth(i - 2, 1, 1))
                    three = "p (s n) -> p s n"
                    dve.tensor_tensor(q_c[:].rearrange(three, s=STEPS), Q[:, 0:BT].rearrange(three, s=STEPS),
                                      turned("q_cos"), ALU.mult)
                    dve.tensor_tensor(q_s[:].rearrange(three, s=STEPS), Q[:, BT:2 * BT].rearrange(three, s=STEPS),
                                      turned("q_sin"), ALU.mult).then_inc(qmul_v, 1)
                if live(i - 3):
                    cell(i - 3, 1)
                if live(i - 2):
                    dve.wait_ge(rsc_mm, nth(i - 2, 1, 1))
                    dve.tensor_tensor(ret_w[:], RSC[:, 0:BT].rearrange("p (t n) -> p t n", t=T),
                                      c("decay").unsqueeze(1).broadcast_to([P, T, P]),
                                      ALU.mult).then_inc(rw_v, 1)
                if live(i - 1):
                    dve.wait_ge(y_mm, nth(i - 1, 1, 1))
                    dve.wait_ge(xb_p, nth(i - 1, 1, 1))
                    dve.tensor_tensor(s1[:].rearrange("p t d -> p (t d)"), Y[:, 0:BT],
                                      x_mlp_b[:].rearrange("p t d -> p (t d)"), ALU.add).then_inc(s1_v, 1)
                    dve.wait_ge(s1_v, nth(i - 1, 1, 1))
                    stats(1, s1, i - 1)
                if live(i):
                    dve.wait_ge(asc_mm, nth(i, 1, 1))
                    dve.tensor_tensor(attn_w[:].rearrange("p t (h n) -> p (t h) n", h=HEADS),
                                      ASC[:].rearrange("p (j n) -> p j n", j=T * HEADS),
                                      c("causal").unsqueeze(1).broadcast_to([P, T * HEADS, P]),
                                      ALU.mult).then_inc(aw_v, 1)
                if live(i - 3):
                    cell(i - 3, 2)
                if live(i - 2):
                    dve.wait_ge(rout_mm, nth(i - 2, 1, 1))
                    dve.tensor_tensor(s2[:].rearrange("p t d -> p (t d)"), ROUT[:, 0:BT],
                                      x1[:].rearrange("p t d -> p (t d)"), ALU.add).then_inc(s2_v, 1)
                    dve.wait_ge(s2_v, nth(i - 2, 1, 1))
                    stats(2, s2, i - 2)
                if live(i - 1):
                    normalise(1, x1, s1, i - 1, x1_v)
                    dve.wait_ge(k_mm, nth(i - 1, 1, 1))
                    dve.tensor_tensor(k_c[:].rearrange(three_dims, s=STEPS), K[:, 0:BT].rearrange(three_dims, s=STEPS),
                                      turned("k_cos"), ALU.mult)
                    dve.tensor_tensor(k_s[:].rearrange(three_dims, s=STEPS),
                                      K[:, BT:2 * BT].rearrange(three_dims, s=STEPS),
                                      turned("k_sin"), ALU.mult).then_inc(kmul_v, 1)
                if live(i - 2):
                    if live(i - 3):
                        dve.wait_ge(keep_p, nth(i - 3, 1, 1))
                    normalise(2, x2, s2, i - 2, x2_v)
                if live(i):
                    dve.wait_ge(xa_in, nth(i, 16, 16))
                    for t in range(T):
                        dve.wait_ge(num_mm, nth(i, T, t + 1))
                        sums = NUM[t][:, 0:HEADS * VW].rearrange("p (h n) -> p h n", h=HEADS)[:, :, D]
                        dve.tensor_scalar(den[:, t, :], sums, FEAT_EPS, None, ALU.add).then_inc(den_v, 1)
                        dve.wait_ge(den_v, nth(i, T, t + 1))
                        dve.reciprocal(rden[:, t, :], den[:, t, :]).then_inc(rden_v, 1)
                        dve.wait_ge(rden_v, nth(i, T, t + 1))
                        dve.scalar_tensor_tensor(u[:, t, :], NUM[t][:, 0:D], rden[:, t, 0:1], x_attn[:, t, :],
                                                 ALU.mult, ALU.add).then_inc(u0_v, 1)
                        dve.wait_ge(u0_v, nth(i, T, t + 1))
                        dve.scalar_tensor_tensor(u[:, t, :], NUM[t][:, VW:VW + D], rden[:, t, 1:2], u[:, t, :],
                                                 ALU.mult, ALU.add).then_inc(u_v, 1)
                    dve.wait_ge(u_v, nth(i, T, T))
                    stats(0, u, i)
                if live(i - 3):
                    cell(i - 3, 3)

            three_dims = "p (s n) -> p s n"
            for i in range(LOOP0):
                body(i)
            with dve.Fori(LOOP0, NB) as i:
                body(i)
            for i in range(NB, LAST):
                body(i)

            dve.wait_ge(state_v, STEPS * NB + 1)
            for n in range(2):
                dve.tensor_copy(state2[:, n, :], state[:]).then_inc(f_st2, 1)
            dve.wait_ge(f_add_mm, 1)
            dve.tensor_copy(add_row[:], bank[2][:, 0:D]).then_inc(f_add, 1)

            def summed(g, odd, first):
                dve.wait_ge(f_tanh, g + 1)
                if not first:
                    dve.wait_ge(f_o, g - 1)
                dve.tensor_tensor(e_s[:, odd, :], x2_all[:, bass.ds(g * (GT * D), GT * D)], e_h[:, odd, :],
                                  ALU.add).then_inc(f_s, 1)
                dve.wait_ge(f_s, g + 1)
                for t in range(GT):
                    ins = dve.bn_stats(e_st[:, odd, t, :], e_s[:, odd, t * D:(t + 1) * D])
                ins.then_inc(f_st, 1)
                dve.wait_ge(f_st, g + 1)
                dve.memset(wait_slot[:], 0.0)
                for t in range(GT):
                    ins = dve.bn_aggr(e_mv[:, odd, t, :], e_st[:, odd, t, :])
                ins.then_inc(f_mv, 1)

            def scaled(g, odd, first):
                dve.wait_ge(f_rs, g + 1)
                if not first:
                    dve.wait_ge(stored[odd], (g - odd) * 8)
                for t in range(GT):
                    r = slice(t * D, (t + 1) * D)
                    ins = dve.tensor_scalar(e_o[:, odd, r], e_s[:, odd, r], e_mv[:, odd, t, 0:1],
                                            e_rs[:, odd, t:t + 1], ALU.subtract, ALU.mult)
                ins.then_inc(f_o, 1)

            summed(0, 0, True)
            summed(1, 1, True)
            scaled(0, 0, True)
            summed(2, 0, False)
            scaled(1, 1, True)
            with dve.Fori(2, NG - 3, 2) as g:
                summed(g + 1, 1, False)
                scaled(g, 0, False)
                summed(g + 2, 0, False)
                scaled(g + 1, 1, False)
            summed(NG - 1, 1, False)
            scaled(NG - 2, 0, False)
            scaled(NG - 1, 1, False)

        @block.gpsimd
        def _(pool):
            pool.wait_ge(w_in, 48)
            for g, (wn_, un_) in enumerate((("wf", "uf"), ("wi", "ui"), ("wc", "uc"))):
                half = 0.5 if g < 2 else 1.0
                pool.tensor_scalar(gate_w[:, g, :], w(wn_), half, 1.0, ALU.mult, ALU.mult)
                pool.tensor_scalar(gate_u[:, g, :], w(un_), 0.5 * half, 1.0, ALU.mult, ALU.mult)
            pool.tensor_scalar(out_u[:], w("uo"), 0.5, 1.0, ALU.mult, ALU.mult).then_inc(prep_pool, 1)
            pool.wait_ge(prep_dve, 1)

            def root(n, b):
                pool.wait_ge(mv_v[n], nth(b, 1, 1))
                pool.tensor_tensor(ve[n][:], mv[n][:, :, 1], ln_eps[:, min(n, 1), 0:T], ALU.add).then_inc(ve_p[n], 1)
                pool.wait_ge(ve_p[n], nth(b, 1, 1))
                pool.tensor_tensor(rstd[n][:], ve[n][:], minus_half[:, 0:T], ALU.pow).then_inc(rs_p[n], 1)

            def body(i):
                if live(i - 1):
                    b = i - 1
                    pool.wait_ge(xb_in, nth(b, 16, 16))
                    if live(b - 1):
                        pool.wait_ge(s1_v, nth(b - 1, 1, 1))
                    pool.tensor_tensor(x_mlp_b[:], x_mlp[:], w("b2").unsqueeze(1).broadcast_to([P, T, D]),
                                       ALU.add).then_inc(xb_p, 1)
                if live(i - 2):
                    pool.wait_ge(qmul_v, nth(i - 2, 1, 1))
                    pool.tensor_tensor(qT[:], q_c[:], q_s[:], ALU.add).then_inc(q_p, 1)
                if live(i - 1):
                    root(1, i - 1)
                if live(i - 2):
                    root(2, i - 2)
                if live(i - 1):
                    pool.wait_ge(kmul_v, nth(i - 1, 1, 1))
                    pool.tensor_tensor(kT[:], k_c[:], k_s[:], ALU.add).then_inc(k_p, 1)
                if live(i - 2):
                    pool.wait_ge(x2_v, nth(i - 2, 1, 1))
                    pool.tensor_copy(x2_all[:, bass.ds((i - 2) * BT, BT)],
                                     x2[:].rearrange("p t d -> p (t d)")).then_inc(keep_p, 1)
                if live(i):
                    root(0, i)

            for i in range(LOOP0):
                body(i)
            with pool.Fori(LOOP0, NB) as i:
                body(i)
            for i in range(NB, LAST):
                body(i)

            pool.wait_ge(f_add, 1)
            pool.wait_ge(zo_v, NB)

            def enter(g, odd, first):
                if not first:
                    pool.wait_ge(f_tanh, g - 1)
                pool.tensor_tensor(e_in[:, odd, :].rearrange("p (t d) -> p t d", t=GT),
                                   zo_all[:, bass.ds(g * (GT * D), GT * D)].rearrange("p (t d) -> p t d", t=GT),
                                   add_row[:].unsqueeze(1).broadcast_to([P, GT, D]), ALU.add).then_inc(f_in, 1)

            def rooted(g, odd):
                pool.wait_ge(f_mv, g + 1)
                pool.tensor_tensor(e_ve[:, odd, :], e_mv[:, odd, :, 1], ln_eps[:, 1, :], ALU.add).then_inc(f_ve, 1)
                pool.wait_ge(f_ve, g + 1)
                pool.tensor_tensor(e_rs[:, odd, :], e_ve[:, odd, :], minus_half[:], ALU.pow).then_inc(f_rs, 1)

            enter(0, 0, True)
            enter(1, 1, True)
            with pool.Fori(0, NG - 3, 2) as g:
                rooted(g, 0)
                enter(g + 2, 0, False)
                rooted(g + 1, 1)
                enter(g + 3, 1, False)
            rooted(NG - 2, 0)
            rooted(NG - 1, 1)


def tables():
    f = np.float32
    pos = np.arange(SEQ, dtype=f)
    half = D // 2
    vec = (np.arange(0, D, 2, dtype=f) + f(0.4 * D)) / f(1.4 * D)
    scale = vec[None, :] ** (pos / f(SCALE_BASE))[:, None]
    freqs = f(1.0) / f(THETA) ** (np.arange(half, dtype=f) / f(half))
    angle = pos[:, None] * freqs[None, :]
    up = lambda a: np.repeat(a, 2, axis=-1).T.astype(f)
    sin, cos = np.sin(angle), np.cos(angle)
    inv = f(1.0) / scale
    r = np.arange(P)
    same = (r[:, None] // SEQ) == (r[None, :] // SEQ)
    later = same & (r[None, :] >= r[:, None])
    diff = (r[None, :] - r[:, None]).astype(f)
    part = np.zeros((P, 3), f)
    part[:3] = np.eye(3)
    return {"ident": np.eye(P), "causal": later, "decay": np.where(later, f(GAMMA) ** np.where(later, diff, 0), 0),
            "q_cos": up(cos * scale), "q_sin": up(sin * scale), "k_cos": up(cos * inv), "k_sin": up(sin * inv),
            "part": part}


def kernel(**inputs):
    import concourse.bacc as _bacc
    from concourse.bass_utils import run_bass_kernel_spmd as _run

    a = {k: np.asarray(v) for k, v in inputs.items()}
    blocks = lambda x: x.reshape(NB, T, P, D).transpose(0, 2, 1, 3).reshape(NB, P, T * D)
    columns = lambda x: x.reshape(NB, BT, D).transpose(0, 2, 1)
    om = a["L0_attn_omega"].T
    pack = {
        "aq_T": a["L0_attn_Wq"].T, "ak_T": a["L0_attn_Wk"].T, "av_T": a["L0_attn_Wv"].T, "ao": a["L0_attn_Wo"],
        "omega_T": np.concatenate([om, om], axis=0), "aq": a["L0_attn_Wq"], "ak": a["L0_attn_Wk"],
        "w1": a["L0_attn_W1"], "w2": a["L0_attn_W2"].reshape(FC, P, D).transpose(1, 0, 2).reshape(P, FC * D),
        "b1": a["L0_attn_b1"].reshape(FC, P).T, "gamma": a["L0_attn_gamma"][:, None],
        "beta": a["L0_attn_beta"][:, None], "b2": np.tile(a["L0_attn_b2"][None, :], (P, 1)),
        "rq": a["L0_xattn_Wq"], "rk": a["L0_xattn_Wk"], "rv": a["L0_xattn_Wv"],
        "wf": a["L0_ffn_wf"].T, "wi": a["L0_ffn_wi"].T, "wc": a["L0_ffn_wc"].T,
        "uf": a["L0_ffn_uf"].T, "ui": a["L0_ffn_ui"].T, "uc": a["L0_ffn_uc"].T,
        "wo": a["L0_ffn_wo"].T, "uo": a["L0_ffn_uo"].T, "c0": a["L0_ffn_in_c"][:, None],
    }
    rows = np.concatenate([a["L0_ffn_bf"], a["L0_ffn_bi"], a["L0_ffn_bc"], a["L0_ffn_bo"]])
    made = tables()
    arrays = {
        "x_rows": blocks(a["x"]), "x_cols": columns(a["x"]), "ctx_cols": columns(a["ctx_1024"]),
        "weights": np.concatenate([pack[n] for n, _ in W_COLS], axis=1),
        "bias_rows": np.tile(rows[None, :], (3, 1)),
        "consts": np.concatenate([made[n].astype(np.float32) for n, _ in C_COLS], axis=1),
    }
    arrays = {k: np.ascontiguousarray(v) for k, v in arrays.items()}
    nc = _bacc.Bacc("TRN2", target_bir_lowering=False, num_devices=1)
    args = [nc.dram_tensor(k, v.shape, F32, kind="ExternalInput").ap() for k, v in arrays.items()]
    out = nc.dram_tensor("out", (NG, P, GT * D), F32, kind="ExternalOutput").ap()
    program(nc, *args, out)
    r = _run(nc, [arrays], core_ids=[0])
    got = r.results[0]["out"]
    return got.reshape(NG, P, GT, D).transpose(0, 2, 1, 3).reshape(SEQS, SEQ, D)
```

```python
from contextlib import ExitStack

import numpy as np
import concourse.bass as bass
from concourse import mybir

F32 = mybir.dt.float32
F32R = mybir.dt.float32r
BF16 = mybir.dt.bfloat16
ALU = mybir.AluOpType
ACT = mybir.ActivationFunctionType
AX = mybir.AxisListType

P = 128
SEQS, SEQ, D = 128, 64, 128
TOKENS = SEQS * SEQ
T = 2
BT = T * P
NB = TOKENS // BT
STEPS = BT // SEQ
HEADS, DH, M = 2, 64, 128
FC = 4
VW = D + 1
GT = 4
GV = 1
NG = TOKENS // (GT * P)

FEAT_EPS = 1e-6
LN_EPS = 1e-5
ATTN_LN_EPS = 1e6
GAMMA, THETA, SCALE_BASE = 0.96875, 10000.0, 512.0

W_COLS = [("aq_T", D), ("ak_T", D), ("av_T", D), ("ao", D), ("omega_T", M), ("aq", D), ("ak", D),
          ("w1", FC * P), ("w2", FC * P), ("b1", FC), ("gamma", 1), ("beta", 1), ("b2", D),
          ("rq", D), ("rk", D), ("rv", D), ("wf", D), ("wi", D), ("wc", D),
          ("uf", D), ("ui", D), ("uc", D), ("wo", D), ("uo", D), ("c0", 1)]
FRONT_COLS = 7 * D
C_COLS = [("ident", P), ("causal", P), ("decay", P), ("q_cos", SEQ), ("q_sin", SEQ),
          ("k_cos", SEQ), ("k_sin", SEQ), ("part", 3)]


def offsets(cols):
    at, where = 0, {}
    for name, n in cols:
        where[name] = (at, at + n)
        at += n
    return where, at


def program(nc, x_rows, x_cols, ctx_cols, weights, bias_rows, consts, out):
    wat, wn = offsets(W_COLS)
    cat, cn = offsets(C_COLS)
    LAST = NB + 3
    LOOP0 = 4
    U = 4
    LOOP1 = LOOP0 + (NB - LOOP0) // U * U
    AHEAD1 = LOOP0 + (NB - 1 - LOOP0) // U * U

    def live(b):
        return not isinstance(b, int) or 0 <= b < NB

    def nth(b, per, k):
        return b * per + k

    with ExitStack() as ctx:
        def sb(name, shape, dt=F32):
            return ctx.enter_context(nc.sbuf_tensor(name, shape, dt))

        def sem(name):
            return ctx.enter_context(nc.semaphore(name))

        wts = sb("wts", [P, wn])
        con = sb("con", [P, cn])
        bias_in = sb("bias_in", [3, 4 * D])
        bias_rest = sb("bias_rest", [3, 4 * D])
        bias_sum = sb("bias_sum", [3, 4 * D])
        bias_piece = sb("bias_piece", [3, 3, 4 * D], BF16)
        bias_parts = sb("bias_parts", [3, 4 * D], BF16)
        ones3 = sb("ones3", [3, BT], BF16)
        split_at, split_n = offsets([("front", 8 * P),
                                     ("w1", FC * P), ("rq", D), ("rq_rot", D), ("rk", D), ("rk_rot", D),
                                     ("gate_w", 3 * D)])
        sw_hi = sb("sw_hi", [P, split_n], F32R)
        sw_lo = sb("sw_lo", [P, split_n], F32R)
        b1 = sb("b1_beta", [P, FC])
        gate_u = sb("gate_u", [P, 3, D])
        out_u = sb("out_u", [P, D])
        ln_eps = sb("ln_eps", [P, 2, 4])
        minus_half = sb("minus_half", [P, 4])

        def w(name):
            return wts[:, wat[name][0]:wat[name][1]]

        def s(name, of):
            return of[:, split_at[name][0]:split_at[name][1]]

        def c(name):
            return con[:, cat[name][0]:cat[name][1]]

        ident = c("ident")

        def front_qk(of, h):
            return s("front", of)[:, 0:4 * P].rearrange("p (j h m) -> p j h m", j=2, h=HEADS)[:, :, h, :]

        def pairs(ap):
            return ap.rearrange("p (n two) -> p n two", two=2)

        def turned(table):
            return c(table).unsqueeze(1).broadcast_to([P, STEPS, SEQ])

        xT = sb("xT", [P, BT])
        x_hi = sb("x_hi", [P, BT], F32R)
        x_lo = sb("x_lo", [P, BT], F32R)
        x_attn = sb("x_attn", [P, T, D])
        x_mlp = sb("x_mlp", [P, T, D])
        x_mlp_b = sb("x_mlp_b", [P, T, D])
        ctxT = sb("ctxT", [P, BT])
        ctx_hi = sb("ctx_hi", [P, BT], F32R)
        ctx_lo = sb("ctx_lo", [P, BT], F32R)
        qk_sq = sb("qk_sq", [P, T, 2 * D])
        z_top = sb("z_top", [P, T, 4])
        sq_sum = sb("sq_sum", [P, T, 4])
        z_max = sb("z_max", [P, T, 4])
        z_bias = sb("z_bias", [P, T, 4])
        feat = sb("feat", [P, T, 4 * M])
        featT = sb("featT", [P, T, 4 * P])
        values = sb("values", [P, T, HEADS, VW])
        attn_w = sb("attn_w", [P, T, HEADS * P])
        den = sb("den", [P, T, HEADS])
        rden = sb("rden", [P, T, HEADS])
        u = sb("u", [P, T, D])
        u_n = sb("u_n", [P, T, D])
        n_hi = sb("n_hi", [P, BT], F32R)
        n_lo = sb("n_lo", [P, BT], F32R)
        hidden = sb("hidden", [P, FC, BT])
        s1 = sb("s1", [P, T, D])
        x1 = sb("x1", [P, T, D])
        x1T = sb("x1T", [P, BT])
        x1_hi = sb("x1_hi", [P, BT], F32R)
        x1_lo = sb("x1_lo", [P, BT], F32R)
        q_c = sb("q_c", [P, BT])
        q_s = sb("q_s", [P, BT])
        qT = sb("qT", [P, BT])
        k_two = sb("k_two", [P, 2 * BT])
        k_c = sb("k_c", [P, BT])
        k_s = sb("k_s", [P, BT])
        kT = sb("kT", [P, BT])
        rv = sb("rv_tok", [P, T, D])
        ret_w = sb("ret_w", [P, T, P])
        s2 = sb("s2", [P, T, D])
        x2 = sb("x2", [P, T, D])
        x2_hi = sb("x2_hi", [P, BT], F32R)
        x2_lo = sb("x2_lo", [P, BT], F32R)
        st = [sb(f"st{n}", [P, T, 6]) for n in range(3)]
        mv = [sb(f"mv{n}", [P, T, 2]) for n in range(3)]
        ve = [sb(f"ve{n}", [P, T]) for n in range(3)]
        rstd = [sb(f"rstd{n}", [P, T]) for n in range(3)]
        state = sb("state", [P, SEQ])
        gates = sb("gates", [P, 3, SEQ])
        keep = sb("keep", [P, SEQ])
        gain = sb("gain", [P, SEQ])
        x2_all = sb("x2_all", [P, TOKENS])
        x2T_all = sb("x2T_all", [P, TOKENS])
        state2 = sb("state2", [P, 2, SEQ])
        add_hi = sb("add_hi", [P, D], F32R)
        add_lo = sb("add_lo", [P, D], F32R)
        ident_r = sb("ident_r", [P, P], F32R)
        e_h = sb("e_h", [P, 2, GT * D])
        e_st = sb("e_st", [P, 4, GT, 6])
        e_mv = sb("e_mv", [P, 4, GT, 2])
        e_ve = sb("e_ve", [P, 4, GT])
        e_rs = sb("e_rs", [P, 4, GT])
        e_nb = sb("e_nb", [P, 4, GT])

        GATE = ctx.enter_context(nc.psum_tensor("gate_banks", [P, 1024], F32))
        bank = [None, None] + [ctx.enter_context(nc.psum_tensor(f"bank{n}", [P, 512], F32)) for n in range(2, 5)]
        pair = ctx.enter_context(nc.psum_tensor("banks56", [P, 2, 512], F32))
        bank += [pair[:, 0, :], pair[:, 1, :], ctx.enter_context(nc.psum_tensor("bank7", [P, 512], F32))]
        Z = [bank[2], bank[4]]
        VQ = [bank[3], bank[5]]
        NORM_T, Q, HID, FEAT_T = bank[6], bank[3], [bank[6], bank[7]], [bank[2], bank[4]]
        RSC, Y, ASC, ROUT, K, V = bank[5], bank[3], bank[6], bank[7], bank[2], bank[4]
        NUM, X1_T, X2_T = [bank[5], bank[6]], bank[3], bank[7]
        BETA = bank[7]
        OUT_Z = [bank[3], bank[4]]

        front_in, con_in, w_in, bias_in_in, xT_in, xa_in, xb_in, ctx_in = (sem(n) for n in (
            "front_in", "con_in", "w_in", "bias_in_in", "xT_in", "xa_in", "xb_in", "ctx_in"))
        (prep_mm, beta_mm, front_hi, front_lo, late_hi, late_lo, prep_pool, bias_chain, bias_ready, state_0) = (
            sem(n) for n in ("prep_mm", "beta_mm", "front_hi", "front_lo", "late_hi", "late_lo", "prep_pool",
                             "bias_chain", "bias_ready", "state_0"))
        (proj_mm, gatex_mm, step_mm, norm_T, q_mm, hid_mm, feat_T, rsc_mm, y_mm, asc_mm,
         rout_mm, k_mm, v_mm, num_mm, x1_T, x2_T) = (sem(n) for n in (
             "proj_mm", "gatex_mm", "step_mm", "norm_T", "q_mm", "hid_mm", "feat_T",
             "rsc_mm", "y_mm", "asc_mm", "rout_mm", "k_mm", "v_mm", "num_mm", "x1_T", "x2_T"))
        (xhi_a, chi_a, sq_a, val_a, exp_a, nhi_a, hid_a, featT_a, v_a, x1T_a, x1hi_a, x2T_a,
         tanh_a, k_a) = (sem(n) for n in (
             "xhi_a", "chi_a", "sq_a", "val_a", "exp_a", "nhi_a", "hid_a", "featT_a", "v_a", "x1T_a",
             "x1hi_a", "x2T_a", "tanh_a", "k_a"))
        (top_v, max_v, bias_v, parts_v, state_v, un_v, qmul_v, rw_v, s1_v, aw_v, s2_v, x1_v,
         den_v, rden_v, u0_v, u_v, x2_v, nlo_v) = (sem(n) for n in (
             "top_v", "max_v", "bias_v", "parts_v", "state_v", "un_v", "qmul_v", "rw_v",
             "s1_v", "aw_v", "s2_v", "x1_v", "den_v", "rden_v", "u0_v", "u_v", "x2_v",
             "nlo_v"))
        st_v = [sem(f"st{n}_v") for n in range(3)]
        mv_v = [sem(f"mv{n}_v") for n in range(3)]
        ve_p = [sem(f"ve{n}_p") for n in range(3)]
        rs_p = [sem(f"rs{n}_p") for n in range(3)]
        q_p, kmul_p, k_p, xb_p, keep_p, xlo_p, clo_p, x1lo_p, x2lo_p = (sem(n) for n in (
            "q_p", "kmul_p", "k_p", "xb_p", "keep_p", "xlo_p", "clo_p", "x1lo_p", "x2lo_p"))
        (f_st2, f_add_mm, f_hi, f_lo, f_z, f_tanh, f_s, f_sp, f_st, f_mv, f_ve, f_rs, f_nb, f_o, f_oa) = (
            sem(n) for n in ("f_st2", "f_add_mm", "f_hi", "f_lo", "f_z", "f_tanh", "f_s", "f_sp",
                             "f_st", "f_mv", "f_ve", "f_rs", "f_nb", "f_o", "f_oa"))
        stored = [sem("f_out0"), sem("f_out1")]

        def group(of, g, t0=0, t1=GT):
            return of[:, bass.ds(g * (GT * D) + t0 * D, (t1 - t0) * D)]

        block = ctx.enter_context(nc.Block())

        @block.sync
        def _(sp):
            sp.dma_start(wts[:, 0:FRONT_COLS], weights[:, 0:FRONT_COLS]).then_inc(front_in, 16)

            def step(j):
                if live(j):
                    b = j
                    if live(b - 1):
                        sp.wait_ge(xlo_p, nth(b - 1, 1, 1))
                    sp.dma_start(xT[:], x_cols[bass.ds(b, 1), :, :].rearrange("o p n -> (o p) n")
                                 ).then_inc(xT_in, 16)
                if live(j - 1):
                    b = j - 1
                    if live(b - 1):
                        sp.wait_ge(u_v, nth(b - 1, 1, 1))
                    sp.dma_start(x_attn[:].rearrange("p t d -> p (t d)"),
                                 x_rows[bass.ds(b, 1), :, :].rearrange("o p n -> (o p) n")
                                 ).then_inc(xa_in, 16)
                if live(j - 2):
                    b = j - 2
                    if live(b - 1):
                        sp.wait_ge(xb_p, nth(b - 1, 1, 1))
                    sp.dma_start(x_mlp[:].rearrange("p t d -> p (t d)"),
                                 x_rows[bass.ds(b, 1), :, :].rearrange("o p n -> (o p) n")
                                 ).then_inc(xb_in, 16)
                    if live(b - 1):
                        sp.wait_ge(v_mm, nth(b - 1, 1, 1))
                    sp.dma_start(ctxT[:], ctx_cols[bass.ds(b, 1), :, :].rearrange("o p n -> (o p) n")
                                 ).then_inc(ctx_in, 16)

            step(0)
            sp.dma_start(con[:], consts).then_inc(con_in, 16)
            sp.dma_start(wts[:, FRONT_COLS:], weights[:, FRONT_COLS:]).then_inc(w_in, 16)
            sp.dma_start(bias_in[:], bias_rows).then_inc(bias_in_in, 16)
            for j in range(1, LOOP0):
                step(j)
            with sp.Fori(LOOP0, NB) as j:
                step(j)
            for j in range(NB, NB + 2):
                step(j)

            def store(g, odd):
                sp.wait_ge(f_o, g + 1)
                sp.wait_ge(f_oa, g + 1)
                sp.dma_start(out[bass.ds(g, 1), :, :].rearrange("o p n -> (o p) n"),
                             group(x2_all, g)).then_inc(stored[odd], 16)

            with sp.Fori(0, NG - 1, 2) as g:
                store(g, 0)
                store(g + 1, 1)
            for odd in range(2):
                sp.wait_ge(stored[odd], 16 * (NG // 2))

        @block.tensor
        def _(pe):
            pe.wait_ge(front_in, 16)
            for h in range(HEADS):
                r = slice(DH * h, DH * h + DH)
                pe.matmul(bank[2 + h][:, 0:P], w("aq_T")[r, :], w("omega_T")[r, :], start=True, stop=True)
                pe.matmul(bank[2 + h][:, P:2 * P], w("ak_T")[r, :], w("omega_T")[r, :], start=True, stop=True)
                pe.matmul(bank[2 + h][:, 2 * P:3 * P], w("av_T")[r, :], w("ao")[r, :],
                          start=True, stop=True).then_inc(prep_mm, 1)
            pe.wait_ge(front_hi, 1)
            pe.wait_ge(front_lo, 1)

            def three(dst, lhs_lo, lhs_hi, rhs_lo, rhs_hi, start=True):
                pe.matmul(dst, lhs_lo, rhs_hi, start=start, stop=False, skip_group_check=not start)
                pe.matmul(dst, lhs_hi, rhs_lo, start=False, stop=False, skip_group_check=not start)
                return pe.matmul(dst, lhs_hi, rhs_hi, start=False, stop=True, skip_group_check=not start)

            def front(b, t):
                if t == 0:
                    pe.wait_ge(xhi_a, nth(b, 1, 1))
                    pe.wait_ge(xlo_p, nth(b, 1, 1))
                if live(b - 2) and t == 0:
                    pe.wait_ge(k_a, nth(b - 2, 1, 1))
                    pe.wait_ge(x1hi_a, nth(b - 2, 1, 1))
                if live(b - 2) and t == 1:
                    pe.wait_ge(v_a, nth(b - 2, 1, 1))
                if live(b - 1) and t == 1:
                    pe.wait_ge(u_v, nth(b - 1, 1, 1))
                r = slice(t * P, (t + 1) * P)
                w_lo, w_hi = s("front", sw_lo), s("front", sw_hi)
                three(Z[t][:], x_lo[:, r], x_hi[:, r], w_lo[:, 0:512], w_hi[:, 0:512])

            def front_rest(t):
                r = slice(t * P, (t + 1) * P)
                w_lo, w_hi = s("front", sw_lo), s("front", sw_hi)
                three(VQ[t][:], x_lo[:, r], x_hi[:, r], w_lo[:, 512:1024], w_hi[:, 512:1024]).then_inc(proj_mm, 1)

            def gates_x(b):
                if live(b - 1):
                    pe.wait_ge(tanh_a, nth(b - 1, STEPS, STEPS))
                for g in range(3):
                    pe.matmul(GATE[:, g * BT:(g + 1) * BT], bias_parts[:, g * D:(g + 1) * D], ones3[:],
                              start=(g != 1), stop=False, skip_group_check=True)
                pe.wait_ge(x2T_a, nth(b, 1, 1))
                for part, moving in ((sw_lo, x2_hi), (sw_hi, x2_lo), (sw_hi, x2_hi)):
                    if moving is x2_lo:
                        pe.wait_ge(x2lo_p, nth(b, 1, 1))
                    for g in range(3):
                        pe.matmul(GATE[:, g * BT:(g + 1) * BT], s("gate_w", part)[:, g * D:(g + 1) * D], moving[:],
                                  start=False, stop=(part is sw_hi and moving is x2_hi), skip_group_check=True)

            def step(b, k):
                if not (isinstance(b, int) and b == 0 and k == 0):
                    pe.wait_ge(state_v, nth(b, STEPS, k))
                for g in range(3):
                    at = g * BT + k * SEQ
                    mm = pe.matmul(GATE[:, at:at + SEQ], gate_u[:, g, :], state[:],
                                   start=False, stop=True, skip_group_check=True)
                mm.then_inc(step_mm, 1)

            def turn(dst, src, done):
                for t in range(T):
                    mm = pe.transpose(dst[:, t * P:(t + 1) * P], src[:, t, :], ident)
                mm.then_inc(done, 1)

            def turn_features(b, t):
                pe.wait_ge(exp_a, nth(b, T, t + 1))
                for j in range(4):
                    mm = pe.transpose(FEAT_T[t][:, j * P:(j + 1) * P], feat[:, t, j * M:(j + 1) * M], ident)
                mm.then_inc(feat_T, 1)

            def queries(i):
                pe.wait_ge(x1lo_p, nth(i - 2, 1, 1))
                if live(i):
                    pe.wait_ge(sq_a, nth(i, T, 1))
                    pe.wait_ge(val_a, nth(i, T, 1))
                three(Q[:, 0:BT], s("rq", sw_lo), s("rq", sw_hi), x1_lo[:], x1_hi[:])
                three(Q[:, BT:2 * BT], s("rq_rot", sw_lo), s("rq_rot", sw_hi), x1_lo[:],
                      x1_hi[:]).then_inc(q_mm, 1)

            def body(i):
                if live(i):
                    front(i, 0)
                    front_rest(0)
                if isinstance(i, int) and i == 3:
                    pe.wait_ge(bias_ready, 1)
                    pe.wait_ge(prep_pool, 1)
                    pe.wait_ge(state_0, 1)
                if live(i - 2) and not live(i):
                    queries(i)
                if live(i - 3):
                    gates_x(i - 3)
                    step(i - 3, 0)
                if live(i):
                    front(i, 1)
                if live(i - 1):
                    pe.wait_ge(un_v, nth(i - 1, 1, 1))
                    turn(NORM_T, u_n, norm_T)
                if live(i):
                    front_rest(1)
                if isinstance(i, int) and i == 0:
                    pe.wait_ge(w_in, 16)
                    for f in range(FC):
                        mm = pe.matmul(BETA[:, f:f + 1], w("w1")[:, f * P:(f + 1) * P], w("beta"),
                                       start=True, stop=True)
                    mm.then_inc(beta_mm, 1)
                    pe.wait_ge(con_in, 16)
                if isinstance(i, int) and i == 1:
                    pe.wait_ge(late_hi, 1)
                    pe.wait_ge(late_lo, 1)
                if live(i - 2) and live(i):
                    queries(i)
                if live(i - 1):
                    pe.wait_ge(nhi_a, nth(i - 1, 1, 1))
                    pe.wait_ge(nlo_v, nth(i - 1, 1, 1))
                    for f in range(FC):
                        r = slice(f * P, (f + 1) * P)
                        mm = three(HID[f // 2][:, (f % 2) * BT:(f % 2 + 1) * BT], s("w1", sw_lo)[:, r],
                                   s("w1", sw_hi)[:, r], n_lo[:], n_hi[:])
                        if f % 2 == 1:
                            mm.then_inc(hid_mm, 1)
                if live(i):
                    turn_features(i, 0)
                if live(i - 3):
                    step(i - 3, 1)
                if live(i - 2):
                    pe.wait_ge(q_p, nth(i - 2, 1, 1))
                    pe.wait_ge(k_p, nth(i - 2, 1, 1))
                    if live(i):
                        pe.wait_ge(sq_a, nth(i, T, 2))
                        pe.wait_ge(val_a, nth(i, T, 2))
                    for t in range(T):
                        r = slice(t * P, (t + 1) * P)
                        mm = pe.matmul(RSC[:, r], kT[:, r], qT[:, r], start=True, stop=True)
                    mm.then_inc(rsc_mm, 1)
                if live(i):
                    turn_features(i, 1)
                if live(i - 1):
                    pe.wait_ge(hid_a, nth(i - 1, FC, FC))
                    for t in range(T):
                        for f in range(FC):
                            mm = pe.matmul(Y[:, t * P:(t + 1) * P], hidden[:, f, t * P:(t + 1) * P],
                                           w("w2")[:, f * P:(f + 1) * P], start=(f == 0), stop=(f == FC - 1))
                    mm.then_inc(y_mm, 1)
                if live(i):
                    pe.wait_ge(featT_a, nth(i, T, T))
                    for t in range(T):
                        for h in range(HEADS):
                            at = (t * HEADS + h) * P
                            mm = pe.matmul(ASC[:, at:at + P], featT[:, t, (HEADS + h) * P:(HEADS + h + 1) * P],
                                           featT[:, t, h * P:(h + 1) * P], start=True, stop=True)
                    mm.then_inc(asc_mm, 1)
                if live(i - 2):
                    pe.wait_ge(rw_v, nth(i - 2, 1, 1))
                    pe.wait_ge(v_a, nth(i - 2, 1, 1))
                    for t in range(T):
                        mm = pe.matmul(ROUT[:, t * P:(t + 1) * P], ret_w[:, t, :], rv[:, t, :],
                                       start=True, stop=True)
                    mm.then_inc(rout_mm, 1)
                if live(i - 3):
                    step(i - 3, 2)
                if live(i - 1):
                    pe.wait_ge(chi_a, nth(i - 1, 1, 1))
                    pe.wait_ge(clo_p, nth(i - 1, 1, 1))
                    three(K[:, 0:BT], s("rk", sw_lo), s("rk", sw_hi), ctx_lo[:], ctx_hi[:])
                    three(K[:, BT:2 * BT], s("rk_rot", sw_lo), s("rk_rot", sw_hi), ctx_lo[:],
                          ctx_hi[:]).then_inc(k_mm, 1)
                    for t in range(T):
                        mm = pe.matmul(V[:, t * P:(t + 1) * P], ctxT[:, t * P:(t + 1) * P], w("rv"),
                                       start=True, stop=True)
                    mm.then_inc(v_mm, 1)
                if live(i):
                    pe.wait_ge(aw_v, nth(i, 1, 1))
                    pe.wait_ge(val_a, nth(i, T, T))
                    for t in range(T):
                        for h in range(HEADS):
                            mm = pe.matmul(NUM[t][:, h * VW:(h + 1) * VW], attn_w[:, t, h * P:(h + 1) * P],
                                           values[:, t, h, :], start=True, stop=True)
                        mm.then_inc(num_mm, 1)
                if live(i - 1):
                    pe.wait_ge(x1_v, nth(i - 1, 1, 1))
                    turn(X1_T, x1, x1_T)
                if live(i - 3):
                    step(i - 3, 3)
                if live(i - 2):
                    pe.wait_ge(x2_v, nth(i - 2, 1, 1))
                    turn(X2_T, x2, x2_T)

            for i in range(LOOP0):
                body(i)
            with pe.Fori(LOOP0, LOOP1 - U + 1, U) as i:
                for n in range(U):
                    body(i + n)
            for i in range(LOOP1, LAST):
                body(i)

            pe.matmul(bank[2][:, 0:D], ones3[:, 0:P], bias_parts[:, 3 * D:4 * D], start=True, stop=False)
            pe.wait_ge(f_st2, 2)
            pe.matmul(bank[2][:, 0:D], state2[:].rearrange("p a b -> p (a b)"), out_u[:],
                      start=False, stop=True).then_inc(f_add_mm, 1)

            def output(g, odd):
                if g >= 2:
                    pe.wait_ge(f_tanh, g - 1)
                for t in range(GT):
                    pe.matmul(OUT_Z[odd][:, t * D:(t + 1) * D], x2T_all[:, (g * GT + t) * P:(g * GT + t + 1) * P],
                              w("wo"), start=(t == 0), stop=False, skip_group_check=True)
                if g == 0:
                    pe.wait_ge(f_hi, 1)
                    pe.wait_ge(f_lo, 1)
                for part in (add_lo, add_hi):
                    mm = pe.matmul(OUT_Z[odd][:].rearrange("p (t d) -> p t d", t=GT), ident_r[:],
                                   part[:].unsqueeze(1).broadcast_to([P, GT, D]),
                                   start=False, stop=(part is add_hi), skip_group_check=True)
                mm.then_inc(f_z, 1)

            for g in range(NG):
                output(g, g % 2)

        @block.scalar
        def _(act):
            def front_parts():
                fw = s("front", sw_hi)
                act.wait_ge(front_in, 16)
                act.activation(fw[:, 6 * P:8 * P], wts[:, wat["aq"][0]:wat["ak"][1]], ACT.Copy)
                for h in range(HEADS):
                    act.wait_ge(prep_mm, h + 1)
                    act.activation(front_qk(sw_hi, h), bank[2 + h][:, 0:2 * P].rearrange("p (j m) -> p j m", j=2),
                                   ACT.Copy, scale=float(DH) ** -0.25)
                    ins = act.activation(fw[:, (4 + h) * P:(5 + h) * P], bank[2 + h][:, 2 * P:3 * P], ACT.Copy)
                    ins.then_inc(front_hi, 1)

            def late_parts():
                act.wait_ge(w_in, 16)
                act.activation(s("w1", sw_hi), w("w1"), ACT.Copy, scale=w("gamma"))
                for name in ("rk", "rq"):
                    act.activation(s(name, sw_hi), w(name), ACT.Copy)
                    src, dst = pairs(w(name)), pairs(s(name + "_rot", sw_hi))
                    act.activation(dst[:, :, 0], src[:, :, 1], ACT.Copy, scale=-1.0)
                    act.activation(dst[:, :, 1], src[:, :, 0], ACT.Copy)
                act.activation(s("gate_w", sw_hi)[:, 0:2 * D], wts[:, wat["wf"][0]:wat["wi"][1]], ACT.Copy, scale=0.5)
                act.activation(s("gate_w", sw_hi)[:, 2 * D:3 * D], w("wc"), ACT.Copy).then_inc(late_hi, 1)

            def squares(b, t):
                act.wait_ge(proj_mm, nth(b, T, t + 1))
                act.activation(qk_sq[:, t, :], VQ[t][:, 2 * P:4 * P], ACT.Square).then_inc(sq_a, 1)
                if live(b - 1):
                    act.wait_ge(num_mm, nth(b - 1, T, t + 1))
                act.activation(values[:, t, :, 0:D], VQ[t][:, 0:2 * P].rearrange("p (h d) -> p h d", h=HEADS),
                               ACT.Copy).then_inc(val_a, 1)

            def features(b, t, js=range(4)):
                if 0 in js:
                    act.wait_ge(bias_v, nth(b, T, t + 1))
                for j in js:
                    ins = act.activation(feat[:, t, j * M:(j + 1) * M], Z[t][:, j * P:(j + 1) * P], ACT.Exp,
                                         bias=z_bias[:, t, j:j + 1])
                if 3 in js:
                    ins.then_inc(exp_a, 1)

            def tanh(b, k):
                act.wait_ge(step_mm, nth(b, STEPS, k + 1))
                view = GATE[:, 0:3 * BT].rearrange("p (g n) -> p g n", g=3)
                act.activation(gates[:], view[:, :, k * SEQ:(k + 1) * SEQ], ACT.Tanh).then_inc(tanh_a, 1)

            def x_part(b):
                act.wait_ge(xT_in, nth(b, 16, 16))
                if live(b - 1):
                    act.wait_ge(proj_mm, nth(b - 1, T, T))
                act.activation(x_hi[:], xT[:], ACT.Copy).then_inc(xhi_a, 1)

            def relu(b, f):
                act.wait_ge(hid_mm, nth(b, 2, f // 2 + 1))
                act.activation(hidden[:, f, :], HID[f // 2][:, (f % 2) * BT:(f % 2 + 1) * BT], ACT.Relu,
                               bias=b1[:, f:f + 1]).then_inc(hid_a, 1)

            def body(i):
                if isinstance(i, int) and i == 0:
                    x_part(0)
                    front_parts()
                if live(i):
                    squares(i, 0)
                if live(i - 3):
                    tanh(i - 3, 0)
                if live(i):
                    features(i, 0, (0, 1))
                if live(i - 1):
                    act.wait_ge(norm_T, nth(i - 1, 1, 1))
                    act.activation(n_hi[:], NORM_T[:, 0:BT], ACT.Copy).then_inc(nhi_a, 1)
                if live(i):
                    features(i, 0, (2, 3))
                    squares(i, 1)
                if live(i - 1):
                    relu(i - 1, 0)
                    relu(i - 1, 1)
                if live(i):
                    features(i, 1)
                if live(i - 1):
                    relu(i - 1, 2)
                    relu(i - 1, 3)
                if live(i - 3):
                    tanh(i - 3, 1)
                if live(i):
                    for t in range(T):
                        act.wait_ge(feat_T, nth(i, T, t + 1))
                        act.activation(featT[:, t, :], FEAT_T[t][:], ACT.Copy, bias=FEAT_EPS,
                                       scale=float(M) ** -0.5).then_inc(featT_a, 1)
                if not (isinstance(i, int) and not live(i + 1)):
                    x_part(i + 1)
                if isinstance(i, int) and i == 0:
                    late_parts()
                if isinstance(i, int) and i == 0:
                    act.wait_ge(late_lo, 1)
                if live(i - 1):
                    act.wait_ge(ctx_in, nth(i - 1, 16, 16))
                    if live(i - 2):
                        act.wait_ge(k_mm, nth(i - 2, 1, 1))
                    act.activation(ctx_hi[:], ctxT[:], ACT.Copy).then_inc(chi_a, 1)
                if live(i - 3):
                    tanh(i - 3, 2)
                if live(i - 1):
                    act.wait_ge(k_mm, nth(i - 1, 1, 1))
                    if live(i - 2):
                        act.wait_ge(kmul_p, nth(i - 2, 1, 1))
                    act.activation(k_two[:], K[:], ACT.Copy).then_inc(k_a, 1)
                    act.wait_ge(v_mm, nth(i - 1, 1, 1))
                    act.activation(rv[:].rearrange("p t d -> p (t d)"), V[:, 0:BT], ACT.Copy).then_inc(v_a, 1)
                    act.wait_ge(x1_T, nth(i - 1, 1, 1))
                    act.activation(x1T[:], X1_T[:, 0:BT], ACT.Copy).then_inc(x1T_a, 1)
                    act.activation(x1_hi[:], X1_T[:, 0:BT], ACT.Copy).then_inc(x1hi_a, 1)
                if live(i - 3):
                    tanh(i - 3, 3)
                if live(i - 2):
                    act.wait_ge(x2_T, nth(i - 2, 1, 1))
                    act.activation(x2_hi[:], X2_T[:, 0:BT], ACT.Copy)
                    act.activation(x2T_all[:, bass.ds((i - 2) * BT, BT)], X2_T[:, 0:BT], ACT.Copy).then_inc(x2T_a, 1)

            for i in range(LOOP0):
                body(i)
            with act.Fori(LOOP0, AHEAD1 - U + 1, U) as i:
                for n in range(U):
                    body(i + n)
            for i in range(AHEAD1, LAST):
                body(i)

            def last(g, n, scaled):
                act.wait_ge(f_z, g + 1)
                if scaled:
                    act.wait_ge(f_nb, g - 2)
                if scaled or g >= 2:
                    act.wait_ge(f_s, g - 1)
                    act.wait_ge(f_sp, g - 1)
                act.activation(e_h[:, n % 2, :], OUT_Z[n % 2][:], ACT.Tanh).then_inc(f_tanh, 1)
                if scaled:
                    scale(g - 3, (n - 3) % 4)

            def scale(g, n):
                for t in range(GV, GT):
                    ins = act.activation(group(x2_all, g, t, t + 1), group(x2_all, g, t, t + 1), ACT.Identity,
                                         bias=e_nb[:, n, t:t + 1], scale=e_rs[:, n, t:t + 1])
                ins.then_inc(f_oa, 1)

            for g in range(4):
                last(g, g, g >= 3)
            with act.Fori(4, NG - 3, 4) as g:
                for n in range(4):
                    last(g + n, n, True)
            for g in range(NG - 3, NG):
                act.wait_ge(f_nb, g + 1)
                scale(g, g % 4)

        @block.vector
        def _(dve):
            for t in range(T):
                nc.vector.memset(values[:, t, :, D:VW], 1.0)
            dve.memset(ones3[:], 1.0)
            dve.memset(minus_half[:], -0.5)
            dve.memset(ln_eps[:, 0, :], ATTN_LN_EPS)
            dve.memset(ln_eps[:, 1, :], LN_EPS)

            def less_hi(name, r, src, scale):
                dst = s(name, sw_lo)[:, r]
                dve.scalar_tensor_tensor(dst, src, scale, s(name, sw_hi)[:, r].bitcast(F32), ALU.mult, ALU.subtract)

            def front_parts():
                for h in range(HEADS):
                    dve.wait_ge(front_hi, h + 1)
                    if h == 0:
                        less_hi("front", slice(6 * P, 8 * P), wts[:, wat["aq"][0]:wat["ak"][1]], 1.0)
                    dve.scalar_tensor_tensor(front_qk(sw_lo, h),
                                             bank[2 + h][:, 0:2 * P].rearrange("p (j m) -> p j m", j=2),
                                             float(DH) ** -0.25, front_qk(sw_hi, h).bitcast(F32),
                                             ALU.mult, ALU.subtract)
                    ins = dve.tensor_tensor(s("front", sw_lo)[:, (4 + h) * P:(5 + h) * P], bank[2 + h][:, 2 * P:3 * P],
                                            s("front", sw_hi)[:, (4 + h) * P:(5 + h) * P].bitcast(F32), ALU.subtract)
                ins.then_inc(front_lo, 1)

            def late_parts():
                dve.wait_ge(beta_mm, 1)
                dve.tensor_tensor(b1[:], BETA[:, 0:FC], w("b1"), ALU.add)
                dve.wait_ge(late_hi, 1)
                less_hi("w1", slice(0, FC * P), w("w1"), w("gamma"))
                for name in ("rk", "rq"):
                    less_hi(name, slice(0, D), w(name), 1.0)
                    src, hi, lo = pairs(w(name)), pairs(s(name + "_rot", sw_hi)), pairs(s(name + "_rot", sw_lo))
                    for n, scale in ((0, -1.0), (1, 1.0)):
                        dve.scalar_tensor_tensor(lo[:, :, n], src[:, :, 1 - n], scale, hi[:, :, n].bitcast(F32),
                                                 ALU.mult, ALU.subtract)
                less_hi("gate_w", slice(0, 2 * D), wts[:, wat["wf"][0]:wat["wi"][1]], 0.5)
                dve.tensor_tensor(s("gate_w", sw_lo)[:, 2 * D:3 * D], w("wc"),
                                  s("gate_w", sw_hi)[:, 2 * D:3 * D].bitcast(F32), ALU.subtract).then_inc(late_lo, 1)

            def split_biases():
                dve.wait_ge(bias_in_in, 16)
                dve.tensor_copy(bias_piece[:, 0, :], bias_in[:]).then_inc(bias_chain, 1)
                dve.memset(state[:], 2.0)
                dve.wait_ge(bias_chain, 1)
                dve.tensor_tensor(bias_rest[:], bias_in[:], bias_piece[:, 0, :], ALU.subtract).then_inc(bias_chain, 1)
                dve.wait_ge(bias_chain, 2)
                dve.tensor_copy(bias_piece[:, 1, :], bias_rest[:]).then_inc(bias_chain, 1)
                dve.tensor_scalar(state[:], state[:], w("c0"), None, ALU.mult).then_inc(state_0, 1)
                dve.wait_ge(bias_chain, 3)
                dve.tensor_tensor(bias_rest[:], bias_rest[:], bias_piece[:, 1, :], ALU.subtract).then_inc(bias_chain, 1)
                dve.wait_ge(bias_chain, 4)
                dve.tensor_copy(bias_piece[:, 2, :], bias_rest[:]).then_inc(bias_chain, 1)

            def place_biases():
                pick = c("part")[0:3, :]
                dve.wait_ge(bias_chain, 5)
                dve.tensor_scalar(bias_sum[:], bias_piece[:, 0, :], pick[:, 0:1], None, ALU.mult).then_inc(bias_chain, 1)
                dve.wait_ge(bias_chain, 6)
                dve.scalar_tensor_tensor(bias_sum[:], bias_piece[:, 1, :], pick[:, 1:2], bias_sum[:], ALU.mult,
                                         ALU.add).then_inc(bias_chain, 1)
                dve.wait_ge(bias_chain, 7)
                dve.scalar_tensor_tensor(bias_sum[:], bias_piece[:, 2, :], pick[:, 2:3], bias_sum[:], ALU.mult,
                                         ALU.add).then_inc(bias_chain, 1)
                dve.wait_ge(bias_chain, 8)
                dve.tensor_scalar(bias_parts[:, 0:2 * D], bias_sum[:, 0:2 * D], 0.5, None, ALU.mult)
                dve.tensor_copy(bias_parts[:, 2 * D:4 * D], bias_sum[:, 2 * D:4 * D]).then_inc(bias_ready, 1)

            front_parts()

            half_scale2 = -0.5 * float(DH) ** -0.5

            def z_tops(b, t):
                dve.wait_ge(proj_mm, nth(b, T, t + 1))
                dve.tensor_reduce(z_top[:, t, :], Z[t][:].rearrange("p (j m) -> p j m", j=4), AX.X, ALU.max)
                dve.wait_ge(sq_a, nth(b, T, t + 1))
                dve.tensor_reduce(sq_sum[:, t, :], qk_sq[:, t, :].rearrange("p (j d) -> p j d", j=4), AX.X,
                                  ALU.add).then_inc(top_v, 1)

            def z_maxima(b, t):
                dve.wait_ge(top_v, nth(b, T, t + 1))
                dve.scalar_tensor_tensor(z_max[:, t, :], sq_sum[:, t, :], half_scale2, z_top[:, t, :],
                                         ALU.mult, ALU.add).then_inc(max_v, 1)

            def z_biases(b, t):
                dve.wait_ge(max_v, nth(b, T, t + 1))
                dve.scalar_tensor_tensor(z_bias[:, t, :], sq_sum[:, t, :], half_scale2, z_max[:, t, :],
                                         ALU.mult, ALU.subtract).then_inc(bias_v, 1)

            def cell_keep(b, k):
                dve.wait_ge(tanh_a, nth(b, STEPS, k + 1))
                dve.scalar_tensor_tensor(keep[:], gates[:, 0, :], 1.0, state[:], ALU.add, ALU.mult)

            def cell_gain(b, k):
                dve.scalar_tensor_tensor(gain[:], gates[:, 1, :], 1.0, gates[:, 2, :], ALU.add,
                                         ALU.mult).then_inc(parts_v, 1)

            def cell_state(b, k):
                dve.wait_ge(parts_v, nth(b, STEPS, k + 1))
                dve.scalar_tensor_tensor(state[:], keep[:], 0.5, gain[:], ALU.mult, ALU.add).then_inc(state_v, 1)

            def row_stats(n, src, b):
                for t in range(T):
                    ins = dve.bn_stats(st[n][:, t, :], src[:, t, :])
                ins.then_inc(st_v[n], 1)

            def mean_var(n, b):
                if isinstance(b, int):
                    dve.wait_ge(st_v[n], nth(b, 1, 1))
                for t in range(T):
                    ins = dve.bn_aggr(mv[n][:, t, :], st[n][:, t, :])
                ins.then_inc(mv_v[n], 1)

            def normalise(n, dst, src, b, t, done):
                if t == 0:
                    dve.wait_ge(rs_p[n], nth(b, 1, 1))
                ins = dve.tensor_scalar(dst[:, t, :], src[:, t, :], mv[n][:, t, 0:1], rstd[n][:, t:t + 1],
                                        ALU.subtract, ALU.mult)
                if t == T - 1:
                    ins.then_inc(done, 1)

            three_dims = "p (s n) -> p s n"

            def turn_queries(b, twin):
                if twin == 0:
                    dve.wait_ge(q_mm, nth(b, 1, 1))
                dst, table = ((q_c, "q_cos"), (q_s, "q_sin"))[twin]
                return dve.tensor_tensor(dst[:].rearrange(three_dims, s=STEPS),
                                         Q[:, twin * BT:(twin + 1) * BT].rearrange(three_dims, s=STEPS),
                                         turned(table), ALU.mult)

            def body(i):
                if live(i - 2) and not live(i):
                    turn_queries(i - 2, 0)
                    turn_queries(i - 2, 1).then_inc(qmul_v, 1)
                if live(i):
                    z_tops(i, 0)
                if live(i - 1):
                    normalise(0, u_n, u, i - 1, 0, un_v)
                if live(i):
                    z_maxima(i, 0)
                if live(i - 1):
                    normalise(0, u_n, u, i - 1, 1, un_v)
                if live(i):
                    z_biases(i, 0)
                if live(i - 3):
                    cell_keep(i - 3, 0)
                    cell_gain(i - 3, 0)
                if live(i - 3):
                    cell_state(i - 3, 0)
                if live(i - 1):
                    dve.wait_ge(nhi_a, nth(i - 1, 1, 1))
                    dve.tensor_tensor(n_lo[:], NORM_T[:, 0:BT], n_hi[:].bitcast(F32), ALU.subtract).then_inc(nlo_v, 1)
                if live(i):
                    z_tops(i, 1)
                if live(i - 2) and live(i):
                    turn_queries(i - 2, 0)
                if live(i):
                    z_maxima(i, 1)
                if live(i - 2) and live(i):
                    turn_queries(i - 2, 1).then_inc(qmul_v, 1)
                if live(i):
                    z_biases(i, 1)
                if live(i - 3):
                    cell_keep(i - 3, 1)
                    cell_gain(i - 3, 1)
                    cell_state(i - 3, 1)
                if live(i - 2):
                    dve.wait_ge(rsc_mm, nth(i - 2, 1, 1))
                    dve.tensor_tensor(ret_w[:], RSC[:, 0:BT].rearrange("p (t n) -> p t n", t=T),
                                      c("decay").unsqueeze(1).broadcast_to([P, T, P]),
                                      ALU.mult).then_inc(rw_v, 1)
                if isinstance(i, int) and i == 1:
                    split_biases()
                if isinstance(i, int) and i == 2:
                    place_biases()
                if live(i - 1):
                    dve.wait_ge(y_mm, nth(i - 1, 1, 1))
                    dve.wait_ge(xb_p, nth(i - 1, 1, 1))
                    dve.tensor_tensor(s1[:].rearrange("p t d -> p (t d)"), Y[:, 0:BT],
                                      x_mlp_b[:].rearrange("p t d -> p (t d)"), ALU.add).then_inc(s1_v, 1)
                    dve.wait_ge(s1_v, nth(i - 1, 1, 1))
                    row_stats(1, s1, i - 1)
                if isinstance(i, int) and i == 0:
                    dve.wait_ge(con_in, 16)
                if live(i):
                    dve.wait_ge(asc_mm, nth(i, 1, 1))
                    dve.tensor_tensor(attn_w[:].rearrange("p t (h n) -> p (t h) n", h=HEADS),
                                      ASC[:].rearrange("p (j n) -> p j n", j=T * HEADS),
                                      c("causal").unsqueeze(1).broadcast_to([P, T * HEADS, P]),
                                      ALU.mult).then_inc(aw_v, 1)
                if isinstance(i, int) and i == 0:
                    late_parts()
                if live(i - 2):
                    dve.wait_ge(rout_mm, nth(i - 2, 1, 1))
                    if live(i - 1):
                        dve.wait_ge(st_v[1], nth(i - 1, 1, 1))
                    dve.tensor_tensor(s2[:].rearrange("p t d -> p (t d)"), ROUT[:, 0:BT],
                                      x1[:].rearrange("p t d -> p (t d)"), ALU.add).then_inc(s2_v, 1)
                if live(i - 1):
                    mean_var(1, i - 1)
                if live(i - 2):
                    dve.wait_ge(s2_v, nth(i - 2, 1, 1))
                    row_stats(2, s2, i - 2)
                if live(i - 3):
                    cell_keep(i - 3, 2)
                    if live(i - 2):
                        dve.wait_ge(st_v[2], nth(i - 2, 1, 1))
                    cell_gain(i - 3, 2)
                if live(i - 2):
                    mean_var(2, i - 2)
                if live(i - 3):
                    cell_state(i - 3, 2)
                if live(i - 1):
                    normalise(1, x1, s1, i - 1, 0, x1_v)
                    normalise(1, x1, s1, i - 1, 1, x1_v)
                if live(i - 2):
                    if live(i - 3):
                        dve.wait_ge(keep_p, nth(i - 3, 1, 1))
                    normalise(2, x2, s2, i - 2, 0, x2_v)
                    normalise(2, x2, s2, i - 2, 1, x2_v)
                if live(i):
                    dve.wait_ge(xa_in, nth(i, 16, 16))
                    dve.wait_ge(num_mm, nth(i, T, T))
                    sums = pair[:, :, 0:HEADS * VW].rearrange("p t (h n) -> p t h n", h=HEADS)[:, :, :, D]
                    dve.tensor_scalar(den[:], sums, FEAT_EPS, None, ALU.add).then_inc(den_v, 1)
                    dve.wait_ge(den_v, nth(i, 1, 1))
                    dve.reciprocal(rden[:], den[:]).then_inc(rden_v, 1)
                    dve.wait_ge(rden_v, nth(i, 1, 1))
                    for t in range(T):
                        dve.scalar_tensor_tensor(u[:, t, :], NUM[t][:, 0:D], rden[:, t, 0:1], x_attn[:, t, :],
                                                 ALU.mult, ALU.add).then_inc(u0_v, 1)
                    for t in range(T):
                        dve.wait_ge(u0_v, nth(i, T, t + 1))
                        ins = dve.scalar_tensor_tensor(u[:, t, :], NUM[t][:, VW:VW + D], rden[:, t, 1:2], u[:, t, :],
                                                       ALU.mult, ALU.add)
                    ins.then_inc(u_v, 1)
                    dve.wait_ge(u_v, nth(i, 1, 1))
                    row_stats(0, u, i)
                if live(i - 3):
                    cell_keep(i - 3, 3)
                    if live(i):
                        dve.wait_ge(st_v[0], nth(i, 1, 1))
                    cell_gain(i - 3, 3)
                if live(i):
                    mean_var(0, i)
                if live(i - 3):
                    cell_state(i - 3, 3)

            for i in range(LOOP0):
                body(i)
            with dve.Fori(LOOP0, LOOP1 - U + 1, U) as i:
                for n in range(U):
                    body(i + n)
            for i in range(LOOP1, LAST):
                body(i)

            dve.wait_ge(state_v, STEPS * NB)
            for n in range(2):
                dve.tensor_copy(state2[:, n, :], state[:]).then_inc(f_st2, 1)
            dve.tensor_copy(ident_r[:], ident)
            dve.wait_ge(f_add_mm, 1)
            dve.tensor_copy(add_hi[:], bank[2][:, 0:D]).then_inc(f_hi, 1)
            dve.wait_ge(f_hi, 1)
            dve.tensor_tensor(add_lo[:], bank[2][:, 0:D], add_hi[:].bitcast(F32), ALU.subtract).then_inc(f_lo, 1)
            dve.wait_ge(keep_p, NB)

            def residual(g, odd, stats_too):
                dve.wait_ge(f_tanh, g + 1)
                if stats_too:
                    dve.wait_ge(f_st, g)
                dve.tensor_tensor(group(x2_all, g, 0, GT - 1), group(x2_all, g, 0, GT - 1),
                                  e_h[:, odd, 0:(GT - 1) * D], ALU.add).then_inc(f_s, 1)

            def moments(g, n):
                for t in range(GT):
                    ins = dve.bn_aggr(e_mv[:, n, t, :], e_st[:, n, t, :])
                ins.then_inc(f_mv, 1)

            def scaled(g, n):
                dve.wait_ge(f_rs, g + 1)
                dve.scalar_tensor_tensor(e_nb[:, n, :], e_mv[:, n, :, 0], -1.0, e_rs[:, n, :],
                                         ALU.mult, ALU.mult).then_inc(f_nb, 1)
                for t in range(GV):
                    ins = dve.tensor_scalar(group(x2_all, g, t, t + 1), group(x2_all, g, t, t + 1),
                                            e_mv[:, n, t, 0:1], e_rs[:, n, t:t + 1], ALU.subtract, ALU.mult)
                ins.then_inc(f_o, 1)

            def summed(g, n):
                for t in range(GT):
                    ins = dve.bn_stats(e_st[:, n, t, :], group(x2_all, g, t, t + 1))
                ins.then_inc(f_st, 1)

            def stage(g, n):
                residual(g, n % 2, n > 0 or not isinstance(g, int) or g > 0)
                if not isinstance(g, int) or g >= 1:
                    moments(g - 1, (n - 1) % 4)
                dve.wait_ge(f_s, g + 1)
                dve.wait_ge(f_sp, g + 1)
                if not isinstance(g, int) or g >= 2:
                    scaled(g - 2, (n - 2) % 4)
                summed(g, n)

            for g in range(4):
                stage(g, g)
            with dve.Fori(4, NG - 3, 4) as g:
                for n in range(4):
                    stage(g + n, n)
            dve.wait_ge(f_st, NG)
            moments(NG - 1, 3)
            scaled(NG - 2, 2)
            scaled(NG - 1, 3)

        @block.gpsimd
        def _(pool):
            def halves():
                pool.wait_ge(con_in, 16)
                pool.wait_ge(w_in, 16)
                for g, un_ in enumerate(("uf", "ui", "uc")):
                    half = 0.5 if g < 2 else 1.0
                    pool.tensor_scalar(gate_u[:, g, :], w(un_), 0.5 * half, 1.0, ALU.mult, ALU.mult)
                pool.tensor_scalar(out_u[:], w("uo"), 0.5, 1.0, ALU.mult, ALU.mult).then_inc(prep_pool, 1)
                pool.wait_ge(front_lo, 1)

            def root(n, b):
                pool.wait_ge(mv_v[n], nth(b, 1, 1))
                pool.tensor_tensor(ve[n][:], mv[n][:, :, 1], ln_eps[:, min(n, 1), 0:T], ALU.add).then_inc(ve_p[n], 1)
                pool.wait_ge(ve_p[n], nth(b, 1, 1))
                pool.tensor_tensor(rstd[n][:], ve[n][:], minus_half[:, 0:T], ALU.pow).then_inc(rs_p[n], 1)

            def x_part(b):
                pool.wait_ge(xhi_a, nth(b, 1, 1))
                pool.tensor_tensor(x_lo[:], xT[:], x_hi[:].bitcast(F32), ALU.subtract).then_inc(xlo_p, 1)

            def keys(b):
                pool.wait_ge(k_a, nth(b, 1, 1))
                three_dims = "p (s n) -> p s n"
                pool.tensor_tensor(k_c[:].rearrange(three_dims, s=STEPS), k_two[:, 0:BT].rearrange(three_dims, s=STEPS),
                                   turned("k_cos"), ALU.mult)
                pool.tensor_tensor(k_s[:].rearrange(three_dims, s=STEPS),
                                   k_two[:, BT:2 * BT].rearrange(three_dims, s=STEPS),
                                   turned("k_sin"), ALU.mult).then_inc(kmul_p, 1)
                pool.wait_ge(kmul_p, nth(b, 1, 1))
                pool.tensor_tensor(kT[:], k_c[:], k_s[:], ALU.add).then_inc(k_p, 1)

            def body(i):
                if isinstance(i, int) and i == 0:
                    x_part(0)
                    halves()
                if live(i - 2):
                    keys(i - 2)
                if live(i - 1):
                    b = i - 1
                    pool.wait_ge(xb_in, nth(b, 16, 16))
                    if live(b - 1):
                        pool.wait_ge(s1_v, nth(b - 1, 1, 1))
                    pool.tensor_tensor(x_mlp_b[:], x_mlp[:], w("b2").unsqueeze(1).broadcast_to([P, T, D]),
                                       ALU.add).then_inc(xb_p, 1)
                if live(i - 2):
                    pool.wait_ge(qmul_v, nth(i - 2, 1, 1))
                    pool.tensor_tensor(qT[:], q_c[:], q_s[:], ALU.add).then_inc(q_p, 1)
                if not (isinstance(i, int) and not live(i + 1)):
                    x_part(i + 1)
                if live(i - 1):
                    pool.wait_ge(chi_a, nth(i - 1, 1, 1))
                    pool.tensor_tensor(ctx_lo[:], ctxT[:], ctx_hi[:].bitcast(F32), ALU.subtract).then_inc(clo_p, 1)
                    root(1, i - 1)
                if live(i - 2):
                    root(2, i - 2)
                if live(i - 1):
                    pool.wait_ge(x1hi_a, nth(i - 1, 1, 1))
                    pool.tensor_tensor(x1_lo[:], x1T[:], x1_hi[:].bitcast(F32), ALU.subtract).then_inc(x1lo_p, 1)
                if live(i - 2):
                    pool.wait_ge(x2T_a, nth(i - 2, 1, 1))
                    pool.tensor_tensor(x2_lo[:], x2T_all[:, bass.ds((i - 2) * BT, BT)], x2_hi[:].bitcast(F32),
                                       ALU.subtract).then_inc(x2lo_p, 1)
                if live(i):
                    root(0, i)
                if live(i - 2):
                    pool.wait_ge(x2_v, nth(i - 2, 1, 1))
                    pool.tensor_copy(x2_all[:, bass.ds((i - 2) * BT, BT)],
                                     x2[:].rearrange("p t d -> p (t d)")).then_inc(keep_p, 1)

            for i in range(LOOP0):
                body(i)
            with pool.Fori(LOOP0, AHEAD1 - U + 1, U) as i:
                for n in range(U):
                    body(i + n)
            for i in range(AHEAD1, LAST):
                body(i)

            def residual(g, odd):
                pool.wait_ge(f_tanh, g + 1)
                pool.tensor_tensor(group(x2_all, g, GT - 1, GT), group(x2_all, g, GT - 1, GT),
                                   e_h[:, odd, (GT - 1) * D:GT * D], ALU.add).then_inc(f_sp, 1)

            def rooted(g, n):
                pool.wait_ge(f_mv, g + 1)
                pool.tensor_tensor(e_ve[:, n, :], e_mv[:, n, :, 1], ln_eps[:, 1, :], ALU.add).then_inc(f_ve, 1)
                pool.wait_ge(f_ve, g + 1)
                pool.tensor_tensor(e_rs[:, n, :], e_ve[:, n, :], minus_half[:], ALU.pow).then_inc(f_rs, 1)

            pool.wait_ge(keep_p, NB)
            residual(0, 0)
            for g in range(1, 5):
                residual(g, g % 2)
                rooted(g - 1, g - 1)
            with pool.Fori(5, NG - 3, 4) as g:
                for n in range(4):
                    residual(g + n, (n + 1) % 2)
                    rooted(g + (n - 1), n)
            for g in range(NG - 3, NG):
                residual(g, g % 2)
                rooted(g - 1, (g - 1) % 4)
            rooted(NG - 1, 3)


def tables():
    f = np.float32
    pos = np.arange(SEQ, dtype=f)
    half = D // 2
    vec = (np.arange(0, D, 2, dtype=f) + f(0.4 * D)) / f(1.4 * D)
    scale = vec[None, :] ** (pos / f(SCALE_BASE))[:, None]
    freqs = f(1.0) / f(THETA) ** (np.arange(half, dtype=f) / f(half))
    angle = pos[:, None] * freqs[None, :]
    up = lambda a: np.repeat(a, 2, axis=-1).T.astype(f)
    sin, cos = np.sin(angle), np.cos(angle)
    inv = f(1.0) / scale
    r = np.arange(P)
    same = (r[:, None] // SEQ) == (r[None, :] // SEQ)
    later = same & (r[None, :] >= r[:, None])
    diff = (r[None, :] - r[:, None]).astype(f)
    part = np.zeros((P, 3), f)
    part[:3] = np.eye(3)
    return {"ident": np.eye(P), "causal": later, "decay": np.where(later, f(GAMMA) ** np.where(later, diff, 0), 0),
            "q_cos": up(cos * scale), "q_sin": up(sin * scale), "k_cos": up(cos * inv), "k_sin": up(sin * inv),
            "part": part}


def kernel(**inputs):
    import concourse.bacc as _bacc
    from concourse.bass_utils import run_bass_kernel_spmd as _run

    a = {k: np.asarray(v) for k, v in inputs.items()}
    blocks = lambda x: x.reshape(NB, T, P, D).transpose(0, 2, 1, 3).reshape(NB, P, T * D)
    columns = lambda x: x.reshape(NB, BT, D).transpose(0, 2, 1)
    om = a["L0_attn_omega"].T
    pack = {
        "aq_T": a["L0_attn_Wq"].T, "ak_T": a["L0_attn_Wk"].T, "av_T": a["L0_attn_Wv"].T, "ao": a["L0_attn_Wo"],
        "omega_T": np.concatenate([om, om], axis=0), "aq": a["L0_attn_Wq"], "ak": a["L0_attn_Wk"],
        "w1": a["L0_attn_W1"], "w2": a["L0_attn_W2"].reshape(FC, P, D).transpose(1, 0, 2).reshape(P, FC * D),
        "b1": a["L0_attn_b1"].reshape(FC, P).T, "gamma": a["L0_attn_gamma"][:, None],
        "beta": a["L0_attn_beta"][:, None], "b2": np.tile(a["L0_attn_b2"][None, :], (P, 1)),
        "rq": a["L0_xattn_Wq"], "rk": a["L0_xattn_Wk"], "rv": a["L0_xattn_Wv"],
        "wf": a["L0_ffn_wf"].T, "wi": a["L0_ffn_wi"].T, "wc": a["L0_ffn_wc"].T,
        "uf": a["L0_ffn_uf"].T, "ui": a["L0_ffn_ui"].T, "uc": a["L0_ffn_uc"].T,
        "wo": a["L0_ffn_wo"].T, "uo": a["L0_ffn_uo"].T, "c0": a["L0_ffn_in_c"][:, None],
    }
    rows = np.concatenate([a["L0_ffn_bf"], a["L0_ffn_bi"], a["L0_ffn_bc"], a["L0_ffn_bo"]])
    made = tables()
    arrays = {
        "x_rows": blocks(a["x"]), "x_cols": columns(a["x"]), "ctx_cols": columns(a["ctx_1024"]),
        "weights": np.concatenate([pack[n] for n, _ in W_COLS], axis=1),
        "bias_rows": np.tile(rows[None, :], (3, 1)),
        "consts": np.concatenate([made[n].astype(np.float32) for n, _ in C_COLS], axis=1),
    }
    arrays = {k: np.ascontiguousarray(v) for k, v in arrays.items()}
    nc = _bacc.Bacc("TRN2", target_bir_lowering=False, num_devices=1)
    args = [nc.dram_tensor(k, v.shape, F32, kind="ExternalInput").ap() for k, v in arrays.items()]
    out = nc.dram_tensor("out", (NG, P, GT * D), F32, kind="ExternalOutput").ap()
    program(nc, *args, out)
    r = _run(nc, [arrays], core_ids=[0])
    got = r.results[0]["out"]
    return got.reshape(NG, P, GT, D).transpose(0, 2, 1, 3).reshape(SEQS, SEQ, D)
```

```python
from contextlib import ExitStack

import numpy as np
import concourse.bass as bass
from concourse import mybir

F32 = mybir.dt.float32
F32R = mybir.dt.float32r
ALU = mybir.AluOpType
ACT = mybir.ActivationFunctionType
AX = mybir.AxisListType

P = 128
SEQS, SEQ, D = 128, 64, 128
TOKENS = SEQS * SEQ
T = 2
BT = T * P
NB = TOKENS // BT
STEPS = BT // SEQ
HEADS, DH, M = 2, 64, 128
FC = 4
VW = D + 1
GT = 4
GV = 1
NG = TOKENS // (GT * P)

FEAT_EPS = 1e-6
LN_EPS = 1e-5
ATTN_LN_EPS = 1e6
GAMMA, THETA, SCALE_BASE = 0.96875, 10000.0, 512.0

W_COLS = [("aq_T", D), ("ak_T", D), ("av_T", D), ("ao", D), ("omega_T", M), ("aq", D), ("ak", D),
          ("w1", FC * P), ("w2", FC * P), ("b1", FC), ("gamma", 1), ("beta", 1), ("b2", D),
          ("rq", D), ("rk", D), ("rv", D), ("wf", D), ("wi", D), ("wc", D),
          ("uf", D), ("ui", D), ("uc", D), ("wo", D), ("uo", D), ("c0", 1), ("gate_b", 3)]
FRONT_COLS = 7 * D
C_COLS = [("ident", P), ("causal", P), ("decay", P), ("q_cos", SEQ), ("q_sin", SEQ),
          ("k_cos", SEQ), ("k_sin", SEQ)]


def offsets(cols):
    at, where = 0, {}
    for name, n in cols:
        where[name] = (at, at + n)
        at += n
    return where, at


def program(nc, x_rows, x_cols, ctx_cols, weights, out_bias, consts, out):
    wat, wn = offsets(W_COLS)
    cat, cn = offsets(C_COLS)
    LAST = NB + 3
    LOOP0 = 4
    U = 4
    LOOP1 = LOOP0 + (NB - LOOP0) // U * U
    AHEAD1 = LOOP0 + (NB - 1 - LOOP0) // U * U

    def live(b):
        return not isinstance(b, int) or 0 <= b < NB

    def last_mlp(i):
        return isinstance(i, int) and i == NB

    def last_retention(i):
        return isinstance(i, int) and i == NB + 1

    def last_recurrence(i):
        return isinstance(i, int) and i == NB + 2

    def nth(b, per, k):
        return b * per + k

    with ExitStack() as ctx:
        def sb(name, shape, dt=F32):
            return ctx.enter_context(nc.sbuf_tensor(name, shape, dt))

        def sem(name):
            return ctx.enter_context(nc.semaphore(name))

        wts = sb("wts", [P, wn])
        con = sb("con", [P, cn])
        bo_row = sb("bo_row", [1, D])
        ones_row = sb("ones_row", [1, P])
        gate_b = sb("gate_b", [P, 3])
        split_at, split_n = offsets([("front", 8 * P),
                                     ("w1", FC * P), ("rq", D), ("rq_rot", D), ("rk", D), ("rk_rot", D),
                                     ("gate_w", 3 * D)])
        sw_hi = sb("sw_hi", [P, split_n], F32R)
        sw_lo = sb("sw_lo", [P, split_n], F32R)
        b1 = sb("b1_beta", [P, FC])
        gate_u = sb("gate_u", [P, 3, D])
        out_u = sb("out_u", [P, D])
        ln_eps = sb("ln_eps", [P, 2, 4])
        minus_half = sb("minus_half", [P, 4])

        def w(name):
            return wts[:, wat[name][0]:wat[name][1]]

        def s(name, of):
            return of[:, split_at[name][0]:split_at[name][1]]

        def c(name):
            return con[:, cat[name][0]:cat[name][1]]

        ident = c("ident")

        def front_qk(of, h):
            return s("front", of)[:, 0:4 * P].rearrange("p (j h m) -> p j h m", j=2, h=HEADS)[:, :, h, :]

        def pairs(ap):
            return ap.rearrange("p (n two) -> p n two", two=2)

        def turned(table):
            return c(table).unsqueeze(1).broadcast_to([P, STEPS, SEQ])

        xT = sb("xT", [P, BT])
        x_hi = sb("x_hi", [P, BT], F32R)
        x_lo = sb("x_lo", [P, BT], F32R)
        x_attn = sb("x_attn", [P, T, D])
        x_mlp = sb("x_mlp", [P, T, D])
        x_mlp_b = sb("x_mlp_b", [P, T, D])
        ctxT = sb("ctxT", [P, BT])
        ctx_hi = sb("ctx_hi", [P, BT], F32R)
        ctx_lo = sb("ctx_lo", [P, BT], F32R)
        qk_sq = sb("qk_sq", [P, T, 2 * D])
        z_top = sb("z_top", [P, T, 4])
        sq_sum = sb("sq_sum", [P, T, 4])
        z_max = sb("z_max", [P, T, 4])
        z_bias = sb("z_bias", [P, T, 4])
        feat = sb("feat", [P, T, 4 * M])
        featT = sb("featT", [P, T, 4 * P])
        values = sb("values", [P, T, HEADS, VW])
        attn_w = sb("attn_w", [P, T, HEADS * P])
        den = sb("den", [P, T, HEADS])
        rden = sb("rden", [P, T, HEADS])
        u = sb("u", [P, T, D])
        u_n = sb("u_n", [P, T, D])
        n_hi = sb("n_hi", [P, BT], F32R)
        n_lo = sb("n_lo", [P, BT], F32R)
        hidden = sb("hidden", [P, FC, BT])
        s1 = sb("s1", [P, T, D])
        x1 = sb("x1", [P, T, D])
        x1T = sb("x1T", [P, BT])
        x1_hi = sb("x1_hi", [P, BT], F32R)
        x1_lo = sb("x1_lo", [P, BT], F32R)
        q_c = sb("q_c", [P, BT])
        q_s = sb("q_s", [P, BT])
        qT = sb("qT", [P, BT])
        k_two = sb("k_two", [P, 2 * BT])
        k_c = sb("k_c", [P, BT])
        k_s = sb("k_s", [P, BT])
        kT = sb("kT", [P, BT])
        rv = sb("rv_tok", [P, T, D])
        ret_w = sb("ret_w", [P, T, P])
        s2 = sb("s2", [P, T, D])
        x2 = sb("x2", [P, T, D])
        x2_hi = sb("x2_hi", [P, BT], F32R)
        x2_lo = sb("x2_lo", [P, BT], F32R)
        st = [sb(f"st{n}", [P, T, 6]) for n in range(3)]
        mv = [sb(f"mv{n}", [P, T, 2]) for n in range(3)]
        ve = [sb(f"ve{n}", [P, T]) for n in range(3)]
        rstd = [sb(f"rstd{n}", [P, T]) for n in range(3)]
        state = sb("state", [P, SEQ])
        gates = sb("gates", [P, 3, SEQ])
        keep = sb("keep", [P, SEQ])
        gain = sb("gain", [P, SEQ])
        x2_all = sb("x2_all", [P, TOKENS])
        x2T_all = sb("x2T_all", [P, TOKENS])
        state2 = sb("state2", [P, 2, SEQ])
        add_hi = sb("add_hi", [P, D], F32R)
        add_lo = sb("add_lo", [P, D], F32R)
        ident_r = sb("ident_r", [P, P], F32R)
        e_h = sb("e_h", [P, 2, GT * D])
        e_st = sb("e_st", [P, 4, GT, 6])
        e_mv = sb("e_mv", [P, 4, GT, 2])
        e_ve = sb("e_ve", [P, 4, GT])
        e_rs = sb("e_rs", [P, 4, GT])
        e_nb = sb("e_nb", [P, 4, GT])

        GATE = ctx.enter_context(nc.psum_tensor("gate_banks", [P, 1024], F32))
        bank = [None, None] + [ctx.enter_context(nc.psum_tensor(f"bank{n}", [P, 512], F32)) for n in range(2, 5)]
        pair = ctx.enter_context(nc.psum_tensor("banks56", [P, 2, 512], F32))
        bank += [pair[:, 0, :], pair[:, 1, :], ctx.enter_context(nc.psum_tensor("bank7", [P, 512], F32))]
        Z = [bank[2], bank[4]]
        VQ = [bank[3], bank[5]]
        NORM_T, Q, HID, FEAT_T = bank[6], bank[3], [bank[6], bank[7]], [bank[2], bank[4]]
        RSC, Y, ASC, ROUT, K, V = bank[5], bank[3], bank[6], bank[7], bank[2], bank[4]
        NUM, X1_T, X2_T = [bank[5], bank[6]], bank[3], bank[7]
        BETA = bank[7]
        OUT_Z = bank[3:7]

        front_in, con_in, w_in, bo_in, xT_in, xa_in, xb_in, ctx_in = (sem(n) for n in (
            "front_in", "con_in", "w_in", "bo_in", "xT_in", "xa_in", "xb_in", "ctx_in"))
        (prep_mm, beta_mm, front_hi, front_lo, late_hi, late_lo, prep_pool, state_2, state_0,
         gates_marked, w1_hi, w1_lo) = (
            sem(n) for n in ("prep_mm", "beta_mm", "front_hi", "front_lo", "late_hi", "late_lo", "prep_pool",
                             "state_2", "state_0", "gates_marked", "w1_hi", "w1_lo"))
        (proj_mm, step_mm, norm_T, q_mm, hid_mm, feat_T, rsc_mm, y_mm, asc_mm,
         rout_mm, k_mm, v_mm, num_mm, x1_T, x2_T) = (sem(n) for n in (
             "proj_mm", "step_mm", "norm_T", "q_mm", "hid_mm", "feat_T",
             "rsc_mm", "y_mm", "asc_mm", "rout_mm", "k_mm", "v_mm", "num_mm", "x1_T", "x2_T"))
        (xhi_a, chi_a, sq_a, val_a, exp_a, nhi_a, hid_a, featT_a, v_a, x1hi_a, x2T_a,
         tanh_a, k_a, gbias_a) = (sem(n) for n in (
             "xhi_a", "chi_a", "sq_a", "val_a", "exp_a", "nhi_a", "hid_a", "featT_a", "v_a",
             "x1hi_a", "x2T_a", "tanh_a", "k_a", "gbias_a"))
        (top_v, max_v, bias_v, parts_v, state_v, un_v, qmul_v, rw_v, s1_v, aw_v, s2_v, x1_v,
         den_v, rden_v, u0_v, u_v, x2_v, nlo_v) = (sem(n) for n in (
             "top_v", "max_v", "bias_v", "parts_v", "state_v", "un_v", "qmul_v", "rw_v",
             "s1_v", "aw_v", "s2_v", "x1_v", "den_v", "rden_v", "u0_v", "u_v", "x2_v",
             "nlo_v"))
        st_v = [sem(f"st{n}_v") for n in range(3)]
        mv_v = [sem(f"mv{n}_v") for n in range(3)]
        ve_p = [sem(f"ve{n}_p") for n in range(3)]
        rs_p = [sem(f"rs{n}_p") for n in range(3)]
        q_p, kmul_p, k_p, xb_p, keep_p, xlo_p, clo_p, x1lo_p, x2lo_p = (sem(n) for n in (
            "q_p", "kmul_p", "k_p", "xb_p", "keep_p", "xlo_p", "clo_p", "x1lo_p", "x2lo_p"))
        (f_st2, f_add_mm, f_hi, f_lo, f_z, f_tanh, f_s, f_sp, f_st, f_mv, f_ve, f_rs, f_nb, f_o, f_oa) = (
            sem(n) for n in ("f_st2", "f_add_mm", "f_hi", "f_lo", "f_z", "f_tanh", "f_s", "f_sp",
                             "f_st", "f_mv", "f_ve", "f_rs", "f_nb", "f_o", "f_oa"))
        stored = [sem("f_out0"), sem("f_out1")]

        def group(of, g, t0=0, t1=GT):
            return of[:, bass.ds(g * (GT * D) + t0 * D, (t1 - t0) * D)]

        block = ctx.enter_context(nc.Block())

        @block.sync
        def _(sp):
            sp.dma_start(wts[:, 0:FRONT_COLS], weights[:, 0:FRONT_COLS]).then_inc(front_in, 16)

            def step(j):
                if live(j):
                    b = j
                    if live(b - 1):
                        sp.wait_ge(xlo_p, nth(b - 1, 1, 1))
                    sp.dma_start(xT[:], x_cols[bass.ds(b, 1), :, :].rearrange("o p n -> (o p) n")
                                 ).then_inc(xT_in, 16)
                if live(j - 1):
                    b = j - 1
                    if live(b - 1):
                        sp.wait_ge(u_v, nth(b - 1, 1, 1))
                    sp.dma_start(x_attn[:].rearrange("p t d -> p (t d)"),
                                 x_rows[bass.ds(b, 1), :, :].rearrange("o p n -> (o p) n")
                                 ).then_inc(xa_in, 16)
                if live(j - 2):
                    b = j - 2
                    if live(b - 1):
                        sp.wait_ge(xb_p, nth(b - 1, 1, 1))
                    sp.dma_start(x_mlp[:].rearrange("p t d -> p (t d)"),
                                 x_rows[bass.ds(b, 1), :, :].rearrange("o p n -> (o p) n")
                                 ).then_inc(xb_in, 16)
                    if live(b - 1):
                        sp.wait_ge(v_mm, nth(b - 1, 1, 1))
                    sp.dma_start(ctxT[:], ctx_cols[bass.ds(b, 1), :, :].rearrange("o p n -> (o p) n")
                                 ).then_inc(ctx_in, 16)

            step(0)
            sp.dma_start(con[:], consts).then_inc(con_in, 16)
            sp.dma_start(wts[:, FRONT_COLS:], weights[:, FRONT_COLS:]).then_inc(w_in, 16)
            sp.dma_start(bo_row[:], out_bias).then_inc(bo_in, 16)
            for j in range(1, LOOP0):
                step(j)
            with sp.Fori(LOOP0, NB) as j:
                step(j)
            for j in range(NB, NB + 2):
                step(j)

            def store(g, odd):
                sp.wait_ge(f_o, g + 1)
                sp.wait_ge(f_oa, g + 1)
                sp.dma_start(out[bass.ds(g, 1), :, :].rearrange("o p n -> (o p) n"),
                             group(x2_all, g)).then_inc(stored[odd], 16)

            with sp.Fori(0, NG - 1, 2) as g:
                store(g, 0)
                store(g + 1, 1)
            for odd in range(2):
                sp.wait_ge(stored[odd], 16 * (NG // 2))

        @block.tensor
        def _(pe):
            pe.wait_ge(front_in, 16)
            for h in range(HEADS):
                r = slice(DH * h, DH * h + DH)
                pe.matmul(bank[2 + h][:, 0:P], w("aq_T")[r, :], w("omega_T")[r, :], start=True, stop=True)
                pe.matmul(bank[2 + h][:, P:2 * P], w("ak_T")[r, :], w("omega_T")[r, :], start=True, stop=True)
                pe.matmul(bank[2 + h][:, 2 * P:3 * P], w("av_T")[r, :], w("ao")[r, :],
                          start=True, stop=True).then_inc(prep_mm, 1)
            pe.wait_ge(front_hi, 1)
            pe.wait_ge(front_lo, 1)

            def three(dst, lhs_lo, lhs_hi, rhs_lo, rhs_hi, start=True):
                pe.matmul(dst, lhs_lo, rhs_hi, start=start, stop=False, skip_group_check=not start)
                pe.matmul(dst, lhs_hi, rhs_lo, start=False, stop=False, skip_group_check=not start)
                return pe.matmul(dst, lhs_hi, rhs_hi, start=False, stop=True, skip_group_check=not start)

            def front(b, t):
                if t == 0:
                    pe.wait_ge(xhi_a, nth(b, 1, 1))
                    pe.wait_ge(xlo_p, nth(b, 1, 1))
                if live(b - 2) and t == 0:
                    pe.wait_ge(k_a, nth(b - 2, 1, 1))
                if live(b - 2) and t == 1:
                    pe.wait_ge(v_a, nth(b - 2, 1, 1))
                r = slice(t * P, (t + 1) * P)
                w_lo, w_hi = s("front", sw_lo), s("front", sw_hi)
                three(Z[t][:], x_lo[:, r], x_hi[:, r], w_lo[:, 0:512], w_hi[:, 0:512])

            def front_rest(b, t):
                if live(b - 2) and t == 0:
                    pe.wait_ge(x1hi_a, nth(b - 2, 1, 1))
                if live(b - 1) and t == 1:
                    pe.wait_ge(u_v, nth(b - 1, 1, 1))
                r = slice(t * P, (t + 1) * P)
                w_lo, w_hi = s("front", sw_lo), s("front", sw_hi)
                pe.matmul(VQ[t][:], x_lo[:, r], w_hi[:, 512:1024], start=True, stop=False)
                pe.matmul(VQ[t][:], x_hi[:, r], w_lo[:, 512:1024], start=False, stop=False)
                if live(b - 1) and t == 1:
                    pe.wait_ge(un_v, nth(b - 1, 1, 1))
                    turn(NORM_T, u_n, norm_T)
                pe.matmul(VQ[t][:], x_hi[:, r], w_hi[:, 512:1024], start=False, stop=True).then_inc(proj_mm, 1)

            def gates_x(b):
                pe.wait_ge(gbias_a, nth(b, 1, 1))
                pe.wait_ge(x2T_a, nth(b, 1, 1))
                for part, moving in ((sw_lo, x2_hi), (sw_hi, x2_lo), (sw_hi, x2_hi)):
                    if moving is x2_lo:
                        pe.wait_ge(x2lo_p, nth(b, 1, 1))
                    for g in range(3):
                        pe.matmul(GATE[:, g * BT:(g + 1) * BT], s("gate_w", part)[:, g * D:(g + 1) * D], moving[:],
                                  start=False, stop=(part is sw_hi and moving is x2_hi), skip_group_check=True)

            def step(b, k):
                if not (isinstance(b, int) and b == 0 and k == 0):
                    pe.wait_ge(state_v, nth(b, STEPS, k))
                for g in range(3):
                    at = g * BT + k * SEQ
                    mm = pe.matmul(GATE[:, at:at + SEQ], gate_u[:, g, :], state[:],
                                   start=False, stop=True, skip_group_check=True)
                mm.then_inc(step_mm, 1)

            def turn(dst, src, done):
                for t in range(T):
                    mm = pe.transpose(dst[:, t * P:(t + 1) * P], src[:, t, :], ident)
                mm.then_inc(done, 1)

            def turn_features(b, t):
                pe.wait_ge(exp_a, nth(b, T, t + 1))
                for j in range(4):
                    mm = pe.transpose(FEAT_T[t][:, j * P:(j + 1) * P], feat[:, t, j * M:(j + 1) * M], ident)
                mm.then_inc(feat_T, 1)

            def queries(i):
                pe.wait_ge(x1lo_p, nth(i - 2, 1, 1))
                if live(i):
                    pe.wait_ge(sq_a, nth(i, T, 1))
                    pe.wait_ge(val_a, nth(i, T, 1))
                three(Q[:, 0:BT], s("rq", sw_lo), s("rq", sw_hi), x1_lo[:], x1_hi[:])
                three(Q[:, BT:2 * BT], s("rq_rot", sw_lo), s("rq_rot", sw_hi), x1_lo[:],
                      x1_hi[:]).then_inc(q_mm, 1)

            def tokens_part(g):
                if g >= 4:
                    pe.wait_ge(f_tanh, g - 3)
                for t in range(GT):
                    pe.matmul(OUT_Z[g % 4][:, t * D:(t + 1) * D], x2T_all[:, (g * GT + t) * P:(g * GT + t + 1) * P],
                              w("wo"), start=(t == 0), stop=False, skip_group_check=True)

            def mlp_second(b, half):
                pe.wait_ge(hid_a, nth(b, FC, 2 * half + 2))
                for f in (2 * half, 2 * half + 1):
                    for t in range(T):
                        mm = pe.matmul(Y[:, t * P:(t + 1) * P], hidden[:, f, t * P:(t + 1) * P],
                                       w("w2")[:, f * P:(f + 1) * P], start=(f == 0 and t == 0),
                                       stop=(f == FC - 1), skip_group_check=True)
                if half == 1:
                    mm.then_inc(y_mm, 1)

            def retention_scores(i):
                pe.wait_ge(q_p, nth(i - 2, 1, 1))
                pe.wait_ge(k_p, nth(i - 2, 1, 1))
                if live(i):
                    pe.wait_ge(sq_a, nth(i, T, 2))
                    pe.wait_ge(val_a, nth(i, T, 2))
                for t in range(T):
                    r = slice(t * P, (t + 1) * P)
                    mm = pe.matmul(RSC[:, r], kT[:, r], qT[:, r], start=True, stop=True)
                mm.then_inc(rsc_mm, 1)

            def retention_output(i):
                pe.wait_ge(rw_v, nth(i - 2, 1, 1))
                pe.wait_ge(v_a, nth(i - 2, 1, 1))
                for t in range(T):
                    mm = pe.matmul(ROUT[:, t * P:(t + 1) * P], ret_w[:, t, :], rv[:, t, :],
                                   start=True, stop=True)
                mm.then_inc(rout_mm, 1)

            def body(i):
                if live(i):
                    front(i, 0)
                    front_rest(i, 0)
                if isinstance(i, int) and i == 3:
                    pe.wait_ge(prep_pool, 1)
                    pe.wait_ge(state_0, 1)
                if live(i - 2) and not live(i):
                    queries(i)
                if live(i):
                    front(i, 1)
                if live(i - 3):
                    gates_x(i - 3)
                    step(i - 3, 0)
                if live(i):
                    front_rest(i, 1)
                elif live(i - 1):
                    pe.wait_ge(un_v, nth(i - 1, 1, 1))
                    turn(NORM_T, u_n, norm_T)
                if isinstance(i, int) and i == 0:
                    pe.wait_ge(w_in, 16)
                    for f in range(FC):
                        mm = pe.matmul(BETA[:, f:f + 1], w("w1")[:, f * P:(f + 1) * P], w("beta"),
                                       start=True, stop=True)
                    mm.then_inc(beta_mm, 1)
                    for r in (slice(0, 512), slice(512, 3 * BT)):
                        mm = pe.matmul(GATE[:, r], s("front", sw_hi)[:, 0:P], s("front", sw_hi)[:, 0:r.stop - r.start],
                                       start=True, stop=True)
                    mm.then_inc(gates_marked, 1)
                    pe.wait_ge(con_in, 16)
                if isinstance(i, int) and i == 1:
                    pe.wait_ge(w1_hi, 1)
                    pe.wait_ge(w1_lo, 1)
                if live(i - 2) and live(i):
                    queries(i)
                if live(i - 3) and live(i):
                    step(i - 3, 1)
                if live(i - 1):
                    pe.wait_ge(nhi_a, nth(i - 1, 1, 1))
                    pe.wait_ge(nlo_v, nth(i - 1, 1, 1))
                    for f in range(FC):
                        r = slice(f * P, (f + 1) * P)
                        mm = three(HID[f // 2][:, (f % 2) * BT:(f % 2 + 1) * BT], s("w1", sw_lo)[:, r],
                                   s("w1", sw_hi)[:, r], n_lo[:], n_hi[:])
                        if f % 2 == 1:
                            mm.then_inc(hid_mm, 1)
                if live(i):
                    turn_features(i, 0)
                if live(i - 3) and not live(i):
                    step(i - 3, 1)
                if last_recurrence(i):
                    tokens_part(0)
                if live(i - 1):
                    if live(i - 2):
                        pe.wait_ge(qmul_v, nth(i - 2, 1, 1))
                    mlp_second(i - 1, 0)
                if live(i - 2):
                    retention_scores(i)
                if last_retention(i):
                    retention_output(i)
                if live(i):
                    turn_features(i, 1)
                if live(i - 1):
                    mlp_second(i - 1, 1)
                if live(i):
                    for t in range(T):
                        pe.wait_ge(featT_a, nth(i, T, t + 1))
                        for h in range(HEADS):
                            at = (t * HEADS + h) * P
                            mm = pe.matmul(ASC[:, at:at + P], featT[:, t, (HEADS + h) * P:(HEADS + h + 1) * P],
                                           featT[:, t, h * P:(h + 1) * P], start=True, stop=True)
                    mm.then_inc(asc_mm, 1)
                if live(i - 3) and not live(i):
                    step(i - 3, 2)
                if last_recurrence(i):
                    tokens_part(1)
                if not live(i) and not last_mlp(i):
                    step(i - 3, 3)
                if last_recurrence(i):
                    tokens_part(2)
                if live(i - 2) and not last_retention(i):
                    retention_output(i)
                if live(i - 3) and live(i):
                    step(i - 3, 2)
                if live(i - 1):
                    if isinstance(i, int) and i == 1:
                        pe.wait_ge(late_hi, 1)
                        pe.wait_ge(late_lo, 1)
                    pe.wait_ge(chi_a, nth(i - 1, 1, 1))
                    pe.wait_ge(clo_p, nth(i - 1, 1, 1))
                    three(K[:, 0:BT], s("rk", sw_lo), s("rk", sw_hi), ctx_lo[:], ctx_hi[:])
                    three(K[:, BT:2 * BT], s("rk_rot", sw_lo), s("rk_rot", sw_hi), ctx_lo[:],
                          ctx_hi[:]).then_inc(k_mm, 1)
                    for t in range(T):
                        mm = pe.matmul(V[:, t * P:(t + 1) * P], ctxT[:, t * P:(t + 1) * P], w("rv"),
                                       start=True, stop=True)
                    mm.then_inc(v_mm, 1)
                if last_mlp(i):
                    step(i - 3, 3)
                if live(i):
                    pe.wait_ge(aw_v, nth(i, 1, 1))
                    pe.wait_ge(val_a, nth(i, T, T))
                    for t in range(T):
                        for h in range(HEADS):
                            mm = pe.matmul(NUM[t][:, h * VW:(h + 1) * VW], attn_w[:, t, h * P:(h + 1) * P],
                                           values[:, t, h, :], start=True, stop=True)
                        mm.then_inc(num_mm, 1)
                if live(i - 1):
                    pe.wait_ge(x1_v, nth(i - 1, 1, 1))
                    turn(X1_T, x1, x1_T)
                if live(i - 3) and live(i):
                    step(i - 3, 3)
                if live(i - 2):
                    pe.wait_ge(x2_v, nth(i - 2, 1, 1))
                    turn(X2_T, x2, x2_T)

            for i in range(LOOP0):
                body(i)
            with pe.Fori(LOOP0, LOOP1 - U + 1, U) as i:
                for n in range(U):
                    body(i + n)
            for i in range(LOOP1, LAST):
                body(i)

            def state_part(g):
                for part in (add_lo, add_hi):
                    mm = pe.matmul(OUT_Z[g % 4][:].rearrange("p (t d) -> p t d", t=GT), ident_r[:],
                                   part[:].unsqueeze(1).broadcast_to([P, GT, D]),
                                   start=False, stop=(part is add_hi), skip_group_check=True)
                mm.then_inc(f_z, 1)

            pe.wait_ge(bo_in, 16)
            pe.matmul(bank[2][:, 0:D], ones_row[:], bo_row[:], start=True, stop=False)
            pe.wait_ge(f_st2, 2)
            pe.matmul(bank[2][:, 0:D], state2[:].rearrange("p a b -> p (a b)"), out_u[:],
                      start=False, stop=True).then_inc(f_add_mm, 1)
            tokens_part(3)
            pe.wait_ge(f_hi, 1)
            pe.wait_ge(f_lo, 1)
            for g in range(4):
                state_part(g)
            for g in range(4, NG):
                tokens_part(g)
                state_part(g)

        @block.scalar
        def _(act):
            def front_parts():
                fw = s("front", sw_hi)
                act.wait_ge(front_in, 16)
                act.activation(fw[:, 6 * P:8 * P], wts[:, wat["aq"][0]:wat["ak"][1]], ACT.Copy)
                for h in range(HEADS):
                    act.wait_ge(prep_mm, h + 1)
                    act.activation(front_qk(sw_hi, h), bank[2 + h][:, 0:2 * P].rearrange("p (j m) -> p j m", j=2),
                                   ACT.Copy, scale=float(DH) ** -0.25)
                    ins = act.activation(fw[:, (4 + h) * P:(5 + h) * P], bank[2 + h][:, 2 * P:3 * P], ACT.Copy)
                    ins.then_inc(front_hi, 1)

            def late_parts():
                act.wait_ge(w_in, 16)
                act.activation(s("w1", sw_hi), w("w1"), ACT.Copy, scale=w("gamma")).then_inc(w1_hi, 1)
                for name in ("rk", "rq"):
                    act.activation(s(name, sw_hi), w(name), ACT.Copy)
                    src, dst = pairs(w(name)), pairs(s(name + "_rot", sw_hi))
                    act.activation(dst[:, :, 0], src[:, :, 1], ACT.Copy, scale=-1.0)
                    act.activation(dst[:, :, 1], src[:, :, 0], ACT.Copy)
                act.activation(s("gate_w", sw_hi)[:, 0:2 * D], wts[:, wat["wf"][0]:wat["wi"][1]], ACT.Copy, scale=0.5)
                act.activation(s("gate_w", sw_hi)[:, 2 * D:3 * D], w("wc"), ACT.Copy).then_inc(late_hi, 1)

            def squares(b, t):
                act.wait_ge(proj_mm, nth(b, T, t + 1))
                act.activation(qk_sq[:, t, :], VQ[t][:, 2 * P:4 * P], ACT.Square).then_inc(sq_a, 1)
                if live(b - 1):
                    act.wait_ge(num_mm, nth(b - 1, T, t + 1))
                act.activation(values[:, t, :, 0:D], VQ[t][:, 0:2 * P].rearrange("p (h d) -> p h d", h=HEADS),
                               ACT.Copy).then_inc(val_a, 1)

            def features(b, t, js=range(4)):
                if 0 in js:
                    act.wait_ge(bias_v, nth(b, T, t + 1))
                for j in js:
                    ins = act.activation(feat[:, t, j * M:(j + 1) * M], Z[t][:, j * P:(j + 1) * P], ACT.Exp,
                                         bias=z_bias[:, t, j:j + 1])
                if 3 in js:
                    ins.then_inc(exp_a, 1)

            def tanh(b, k):
                act.wait_ge(step_mm, nth(b, STEPS, k + 1))
                view = GATE[:, 0:3 * BT].rearrange("p (g n) -> p g n", g=3)
                act.activation(gates[:], view[:, :, k * SEQ:(k + 1) * SEQ], ACT.Tanh).then_inc(tanh_a, 1)

            def gate_biases(b):
                if live(b - 1):
                    act.wait_ge(tanh_a, nth(b - 1, STEPS, STEPS))
                act.activation(GATE[:, 0:3 * BT].rearrange("p (g n) -> p g n", g=3),
                               gate_b[:].unsqueeze(2).broadcast_to([P, 3, BT]), ACT.Copy).then_inc(gbias_a, 1)

            def x_part(b):
                act.wait_ge(xT_in, nth(b, 16, 16))
                if live(b - 1):
                    act.wait_ge(proj_mm, nth(b - 1, T, T))
                act.activation(x_hi[:], xT[:], ACT.Copy).then_inc(xhi_a, 1)

            def relu(b, f):
                if isinstance(b, int) and b == 0:
                    act.wait_ge(w1_lo, 1)
                act.wait_ge(hid_mm, nth(b, 2, f // 2 + 1))
                act.activation(hidden[:, f, :], HID[f // 2][:, (f % 2) * BT:(f % 2 + 1) * BT], ACT.Relu,
                               bias=b1[:, f:f + 1]).then_inc(hid_a, 1)

            def body(i):
                if isinstance(i, int) and i == 0:
                    x_part(0)
                    front_parts()
                if live(i):
                    squares(i, 0)
                if live(i - 3):
                    tanh(i - 3, 0)
                if live(i):
                    features(i, 0, (0, 1))
                if live(i - 1):
                    act.wait_ge(norm_T, nth(i - 1, 1, 1))
                    act.activation(n_hi[:], NORM_T[:, 0:BT], ACT.Copy).then_inc(nhi_a, 1)
                if live(i):
                    features(i, 0, (2, 3))
                    squares(i, 1)
                if live(i - 1):
                    relu(i - 1, 0)
                    relu(i - 1, 1)
                if live(i):
                    features(i, 1)
                if live(i - 1):
                    relu(i - 1, 2)
                    relu(i - 1, 3)
                if live(i - 3):
                    tanh(i - 3, 1)
                if live(i):
                    for t in range(T):
                        act.wait_ge(feat_T, nth(i, T, t + 1))
                        act.activation(featT[:, t, :], FEAT_T[t][:], ACT.Copy, bias=FEAT_EPS,
                                       scale=float(M) ** -0.5).then_inc(featT_a, 1)
                if live(i - 1):
                    act.wait_ge(ctx_in, nth(i - 1, 16, 16))
                    if live(i - 2):
                        act.wait_ge(k_mm, nth(i - 2, 1, 1))
                    act.activation(ctx_hi[:], ctxT[:], ACT.Copy).then_inc(chi_a, 1)
                if not (isinstance(i, int) and not live(i + 1)):
                    x_part(i + 1)
                if isinstance(i, int) and i == 0:
                    late_parts()
                if live(i - 3):
                    tanh(i - 3, 2)
                if live(i - 1):
                    act.wait_ge(k_mm, nth(i - 1, 1, 1))
                    if live(i - 2):
                        act.wait_ge(kmul_p, nth(i - 2, 1, 1))
                    act.activation(k_two[:], K[:], ACT.Copy).then_inc(k_a, 1)
                    act.wait_ge(v_mm, nth(i - 1, 1, 1))
                    act.activation(rv[:].rearrange("p t d -> p (t d)"), V[:, 0:BT], ACT.Copy).then_inc(v_a, 1)
                    if last_mlp(i):
                        tanh(i - 3, 3)
                    act.wait_ge(x1_T, nth(i - 1, 1, 1))
                    act.activation(x1T[:], X1_T[:, 0:BT], ACT.Copy)
                    act.activation(x1_hi[:], X1_T[:, 0:BT], ACT.Copy).then_inc(x1hi_a, 1)
                if live(i - 3) and not last_mlp(i):
                    tanh(i - 3, 3)
                if live(i - 2):
                    act.wait_ge(x2_T, nth(i - 2, 1, 1))
                    act.activation(x2_hi[:], X2_T[:, 0:BT], ACT.Copy)
                    act.activation(x2T_all[:, bass.ds((i - 2) * BT, BT)], X2_T[:, 0:BT], ACT.Copy).then_inc(x2T_a, 1)
                if isinstance(i, int) and i == 2:
                    act.wait_ge(gates_marked, 1)
                    act.wait_ge(late_lo, 1)
                if live(i - 2):
                    gate_biases(i - 2)

            for i in range(LOOP0):
                body(i)
            with act.Fori(LOOP0, AHEAD1 - U + 1, U) as i:
                for n in range(U):
                    body(i + n)
            for i in range(AHEAD1, LAST):
                body(i)

            def last(g, n, scaled):
                act.wait_ge(f_z, g + 1)
                if scaled:
                    act.wait_ge(f_nb, g - 2)
                if scaled or g >= 2:
                    act.wait_ge(f_s, g - 1)
                    act.wait_ge(f_sp, g - 1)
                act.activation(e_h[:, n % 2, :], OUT_Z[n][:], ACT.Tanh).then_inc(f_tanh, 1)
                if scaled:
                    scale(g - 3, (n - 3) % 4)

            def scale(g, n):
                for t in range(GV, GT):
                    ins = act.activation(group(x2_all, g, t, t + 1), group(x2_all, g, t, t + 1), ACT.Identity,
                                         bias=e_nb[:, n, t:t + 1], scale=e_rs[:, n, t:t + 1])
                ins.then_inc(f_oa, 1)

            for g in range(4):
                last(g, g, g >= 3)
            with act.Fori(4, NG - 3, 4) as g:
                for n in range(4):
                    last(g + n, n, True)
            for g in range(NG - 3, NG):
                act.wait_ge(f_nb, g + 1)
                scale(g, g % 4)

        @block.vector
        def _(dve):
            for t in range(T):
                nc.vector.memset(values[:, t, :, D:VW], 1.0)
            dve.memset(ones_row[:], 1.0)
            dve.memset(minus_half[:], -0.5)
            dve.memset(ln_eps[:, 0, :], ATTN_LN_EPS)
            dve.memset(ln_eps[:, 1, :], LN_EPS)

            def less_hi(name, r, src, scale):
                dst = s(name, sw_lo)[:, r]
                return dve.scalar_tensor_tensor(dst, src, scale, s(name, sw_hi)[:, r].bitcast(F32),
                                                ALU.mult, ALU.subtract)

            def front_parts():
                for h in range(HEADS):
                    dve.wait_ge(front_hi, h + 1)
                    if h == 0:
                        less_hi("front", slice(6 * P, 8 * P), wts[:, wat["aq"][0]:wat["ak"][1]], 1.0)
                    dve.scalar_tensor_tensor(front_qk(sw_lo, h),
                                             bank[2 + h][:, 0:2 * P].rearrange("p (j m) -> p j m", j=2),
                                             float(DH) ** -0.25, front_qk(sw_hi, h).bitcast(F32),
                                             ALU.mult, ALU.subtract)
                    ins = dve.tensor_tensor(s("front", sw_lo)[:, (4 + h) * P:(5 + h) * P], bank[2 + h][:, 2 * P:3 * P],
                                            s("front", sw_hi)[:, (4 + h) * P:(5 + h) * P].bitcast(F32), ALU.subtract)
                ins.then_inc(front_lo, 1)

            def first_layer_parts():
                dve.wait_ge(beta_mm, 1)
                dve.tensor_tensor(b1[:], BETA[:, 0:FC], w("b1"), ALU.add)
                dve.wait_ge(w1_hi, 1)
                dve.scalar_tensor_tensor(s("w1", sw_lo), w("w1"), w("gamma"), s("w1", sw_hi).bitcast(F32),
                                         ALU.mult, ALU.subtract).then_inc(w1_lo, 1)

            def late_parts():
                dve.memset(state[:], 2.0).then_inc(state_2, 1)
                dve.tensor_scalar(gate_b[:, 0:2], w("gate_b")[:, 0:2], 0.5, None, ALU.mult)
                dve.tensor_copy(gate_b[:, 2:3], w("gate_b")[:, 2:3])
                dve.wait_ge(late_hi, 1)
                for name in ("rk", "rq"):
                    less_hi(name, slice(0, D), w(name), 1.0)
                    src, hi, lo = pairs(w(name)), pairs(s(name + "_rot", sw_hi)), pairs(s(name + "_rot", sw_lo))
                    for n, scale in ((0, -1.0), (1, 1.0)):
                        dve.scalar_tensor_tensor(lo[:, :, n], src[:, :, 1 - n], scale, hi[:, :, n].bitcast(F32),
                                                 ALU.mult, ALU.subtract)
                dve.wait_ge(state_2, 1)
                dve.tensor_scalar(state[:], state[:], w("c0"), None, ALU.mult).then_inc(state_0, 1)
                less_hi("gate_w", slice(0, 2 * D), wts[:, wat["wf"][0]:wat["wi"][1]], 0.5)
                less_hi("gate_w", slice(2 * D, 3 * D), w("wc"), 1.0).then_inc(late_lo, 1)

            front_parts()

            half_scale2 = -0.5 * float(DH) ** -0.5

            def z_tops(b, t):
                dve.wait_ge(proj_mm, nth(b, T, t + 1))
                dve.tensor_reduce(z_top[:, t, :], Z[t][:].rearrange("p (j m) -> p j m", j=4), AX.X, ALU.max)
                dve.wait_ge(sq_a, nth(b, T, t + 1))
                dve.tensor_reduce(sq_sum[:, t, :], qk_sq[:, t, :].rearrange("p (j d) -> p j d", j=4), AX.X,
                                  ALU.add).then_inc(top_v, 1)

            def z_maxima(b, t):
                dve.wait_ge(top_v, nth(b, T, t + 1))
                dve.scalar_tensor_tensor(z_max[:, t, :], sq_sum[:, t, :], half_scale2, z_top[:, t, :],
                                         ALU.mult, ALU.add).then_inc(max_v, 1)

            def z_biases(b, t):
                dve.wait_ge(max_v, nth(b, T, t + 1))
                dve.scalar_tensor_tensor(z_bias[:, t, :], sq_sum[:, t, :], half_scale2, z_max[:, t, :],
                                         ALU.mult, ALU.subtract).then_inc(bias_v, 1)

            def cell_keep(b, k):
                dve.wait_ge(tanh_a, nth(b, STEPS, k + 1))
                dve.scalar_tensor_tensor(keep[:], gates[:, 0, :], 1.0, state[:], ALU.add, ALU.mult)

            def cell_gain(b, k):
                dve.scalar_tensor_tensor(gain[:], gates[:, 1, :], 1.0, gates[:, 2, :], ALU.add,
                                         ALU.mult).then_inc(parts_v, 1)

            def cell_state(b, k):
                dve.wait_ge(parts_v, nth(b, STEPS, k + 1))
                dve.scalar_tensor_tensor(state[:], keep[:], 0.5, gain[:], ALU.mult, ALU.add).then_inc(state_v, 1)

            def row_stats(n, src, b):
                for t in range(T):
                    ins = dve.bn_stats(st[n][:, t, :], src[:, t, :])
                ins.then_inc(st_v[n], 1)

            def mean_var(n, b):
                if isinstance(b, int):
                    dve.wait_ge(st_v[n], nth(b, 1, 1))
                for t in range(T):
                    ins = dve.bn_aggr(mv[n][:, t, :], st[n][:, t, :])
                ins.then_inc(mv_v[n], 1)

            def normalise(n, dst, src, b, t, done):
                if t == 0:
                    dve.wait_ge(rs_p[n], nth(b, 1, 1))
                ins = dve.tensor_scalar(dst[:, t, :], src[:, t, :], mv[n][:, t, 0:1], rstd[n][:, t:t + 1],
                                        ALU.subtract, ALU.mult)
                if t == T - 1:
                    ins.then_inc(done, 1)

            three_dims = "p (s n) -> p s n"

            def decayed(b):
                dve.wait_ge(rsc_mm, nth(b, 1, 1))
                dve.tensor_tensor(ret_w[:], RSC[:, 0:BT].rearrange("p (t n) -> p t n", t=T),
                                  c("decay").unsqueeze(1).broadcast_to([P, T, P]), ALU.mult).then_inc(rw_v, 1)

            def retained(b):
                dve.wait_ge(rout_mm, nth(b, 1, 1))
                dve.tensor_tensor(s2[:].rearrange("p t d -> p (t d)"), ROUT[:, 0:BT],
                                  x1[:].rearrange("p t d -> p (t d)"), ALU.add).then_inc(s2_v, 1)
                dve.wait_ge(s2_v, nth(b, 1, 1))
                row_stats(2, s2, b)

            def turn_queries(b, twin):
                if twin == 0:
                    dve.wait_ge(q_mm, nth(b, 1, 1))
                dst, table = ((q_c, "q_cos"), (q_s, "q_sin"))[twin]
                return dve.tensor_tensor(dst[:].rearrange(three_dims, s=STEPS),
                                         Q[:, twin * BT:(twin + 1) * BT].rearrange(three_dims, s=STEPS),
                                         turned(table), ALU.mult)

            def body(i):
                if live(i - 2) and not live(i):
                    turn_queries(i - 2, 0)
                    turn_queries(i - 2, 1).then_inc(qmul_v, 1)
                if live(i):
                    z_tops(i, 0)
                if live(i - 1):
                    normalise(0, u_n, u, i - 1, 0, un_v)
                if live(i):
                    z_maxima(i, 0)
                if live(i - 1):
                    normalise(0, u_n, u, i - 1, 1, un_v)
                if live(i):
                    z_biases(i, 0)
                if live(i - 3):
                    cell_keep(i - 3, 0)
                    cell_gain(i - 3, 0)
                    cell_state(i - 3, 0)
                if live(i - 1):
                    dve.wait_ge(nhi_a, nth(i - 1, 1, 1))
                    dve.tensor_tensor(n_lo[:], NORM_T[:, 0:BT], n_hi[:].bitcast(F32), ALU.subtract).then_inc(nlo_v, 1)
                if live(i):
                    z_tops(i, 1)
                if live(i - 2) and live(i):
                    turn_queries(i - 2, 0)
                if live(i):
                    z_maxima(i, 1)
                if live(i - 2) and live(i):
                    turn_queries(i - 2, 1).then_inc(qmul_v, 1)
                if live(i):
                    z_biases(i, 1)
                if last_retention(i):
                    decayed(i - 2)
                if live(i - 3):
                    cell_keep(i - 3, 1)
                    cell_gain(i - 3, 1)
                    cell_state(i - 3, 1)
                if last_retention(i):
                    retained(i - 2)
                    mean_var(2, i - 2)
                if live(i - 2) and not last_retention(i):
                    decayed(i - 2)
                if isinstance(i, int) and i == 1:
                    late_parts()
                if live(i - 1):
                    dve.wait_ge(y_mm, nth(i - 1, 1, 1))
                    dve.wait_ge(xb_p, nth(i - 1, 1, 1))
                    dve.tensor_tensor(s1[:].rearrange("p t d -> p (t d)"), Y[:, 0:BT],
                                      x_mlp_b[:].rearrange("p t d -> p (t d)"), ALU.add).then_inc(s1_v, 1)
                    dve.wait_ge(s1_v, nth(i - 1, 1, 1))
                    row_stats(1, s1, i - 1)
                if isinstance(i, int) and i == 0:
                    dve.wait_ge(con_in, 16)
                if live(i):
                    dve.wait_ge(asc_mm, nth(i, 1, 1))
                    dve.tensor_tensor(attn_w[:].rearrange("p t (h n) -> p (t h) n", h=HEADS),
                                      ASC[:].rearrange("p (j n) -> p j n", j=T * HEADS),
                                      c("causal").unsqueeze(1).broadcast_to([P, T * HEADS, P]),
                                      ALU.mult).then_inc(aw_v, 1)
                if isinstance(i, int) and i == 0:
                    first_layer_parts()
                if last_mlp(i):
                    mean_var(1, i - 1)
                if live(i - 2) and not last_retention(i):
                    dve.wait_ge(rout_mm, nth(i - 2, 1, 1))
                    if live(i - 1):
                        dve.wait_ge(st_v[1], nth(i - 1, 1, 1))
                    dve.tensor_tensor(s2[:].rearrange("p t d -> p (t d)"), ROUT[:, 0:BT],
                                      x1[:].rearrange("p t d -> p (t d)"), ALU.add).then_inc(s2_v, 1)
                if live(i - 1) and not last_mlp(i):
                    mean_var(1, i - 1)
                if live(i - 2) and not last_retention(i):
                    dve.wait_ge(s2_v, nth(i - 2, 1, 1))
                    row_stats(2, s2, i - 2)
                    if last_mlp(i):
                        mean_var(2, i - 2)
                if live(i - 3):
                    cell_keep(i - 3, 2)
                    if live(i - 2):
                        dve.wait_ge(st_v[2], nth(i - 2, 1, 1))
                    cell_gain(i - 3, 2)
                if live(i - 2) and live(i):
                    mean_var(2, i - 2)
                if live(i - 3):
                    cell_state(i - 3, 2)
                if live(i - 1):
                    normalise(1, x1, s1, i - 1, 0, x1_v)
                    normalise(1, x1, s1, i - 1, 1, x1_v)
                if live(i - 2):
                    if live(i - 3):
                        dve.wait_ge(keep_p, nth(i - 3, 1, 1))
                    normalise(2, x2, s2, i - 2, 0, x2_v)
                    normalise(2, x2, s2, i - 2, 1, x2_v)
                if live(i):
                    dve.wait_ge(xa_in, nth(i, 16, 16))
                    dve.wait_ge(num_mm, nth(i, T, T))
                    sums = pair[:, :, 0:HEADS * VW].rearrange("p t (h n) -> p t h n", h=HEADS)[:, :, :, D]
                    dve.tensor_scalar(den[:], sums, FEAT_EPS, None, ALU.add).then_inc(den_v, 1)
                    dve.wait_ge(den_v, nth(i, 1, 1))
                    dve.reciprocal(rden[:], den[:]).then_inc(rden_v, 1)
                    dve.wait_ge(rden_v, nth(i, 1, 1))
                    for t in range(T):
                        dve.scalar_tensor_tensor(u[:, t, :], NUM[t][:, 0:D], rden[:, t, 0:1], x_attn[:, t, :],
                                                 ALU.mult, ALU.add).then_inc(u0_v, 1)
                    for t in range(T):
                        dve.wait_ge(u0_v, nth(i, T, t + 1))
                        ins = dve.scalar_tensor_tensor(u[:, t, :], NUM[t][:, VW:VW + D], rden[:, t, 1:2], u[:, t, :],
                                                       ALU.mult, ALU.add)
                    ins.then_inc(u_v, 1)
                    dve.wait_ge(u_v, nth(i, 1, 1))
                    row_stats(0, u, i)
                if live(i - 3):
                    cell_keep(i - 3, 3)
                    if live(i):
                        dve.wait_ge(st_v[0], nth(i, 1, 1))
                    cell_gain(i - 3, 3)
                if live(i):
                    mean_var(0, i)
                if live(i - 3):
                    cell_state(i - 3, 3)

            for i in range(LOOP0):
                body(i)
            with dve.Fori(LOOP0, LOOP1 - U + 1, U) as i:
                for n in range(U):
                    body(i + n)
            for i in range(LOOP1, LAST):
                body(i)

            dve.wait_ge(state_v, STEPS * NB)
            for n in range(2):
                dve.tensor_copy(state2[:, n, :], state[:]).then_inc(f_st2, 1)
            dve.tensor_copy(ident_r[:], ident)
            dve.wait_ge(f_add_mm, 1)
            dve.tensor_copy(add_hi[:], bank[2][:, 0:D]).then_inc(f_hi, 1)
            dve.wait_ge(f_hi, 1)
            dve.tensor_tensor(add_lo[:], bank[2][:, 0:D], add_hi[:].bitcast(F32), ALU.subtract).then_inc(f_lo, 1)
            dve.wait_ge(keep_p, NB)

            def residual(g, odd, stats_too):
                dve.wait_ge(f_tanh, g + 1)
                if stats_too:
                    dve.wait_ge(f_st, g)
                dve.tensor_tensor(group(x2_all, g, 0, GT - 1), group(x2_all, g, 0, GT - 1),
                                  e_h[:, odd, 0:(GT - 1) * D], ALU.add).then_inc(f_s, 1)

            def moments(g, n):
                for t in range(GT):
                    ins = dve.bn_aggr(e_mv[:, n, t, :], e_st[:, n, t, :])
                ins.then_inc(f_mv, 1)

            def scale_bias(g, n):
                dve.wait_ge(f_rs, g + 1)
                dve.scalar_tensor_tensor(e_nb[:, n, :], e_mv[:, n, :, 0], -1.0, e_rs[:, n, :],
                                         ALU.mult, ALU.mult).then_inc(f_nb, 1)

            def scaled(g, n):
                for t in range(GV):
                    ins = dve.tensor_scalar(group(x2_all, g, t, t + 1), group(x2_all, g, t, t + 1),
                                            e_mv[:, n, t, 0:1], e_rs[:, n, t:t + 1], ALU.subtract, ALU.mult)
                ins.then_inc(f_o, 1)

            def summed(g, n):
                for t in range(GT):
                    ins = dve.bn_stats(e_st[:, n, t, :], group(x2_all, g, t, t + 1))
                ins.then_inc(f_st, 1)

            def stage(g, n):
                loop = not isinstance(g, int)
                residual(g, n % 2, loop or g > 0)
                if loop or g >= 1:
                    moments(g - 1, (n - 1) % 4)
                dve.wait_ge(f_s, g + 1)
                dve.wait_ge(f_sp, g + 1)
                if loop or g >= 2:
                    scale_bias(g - 2, (n - 2) % 4)
                summed(g, n)
                if loop or g >= 2:
                    scaled(g - 2, (n - 2) % 4)

            for g in range(4):
                stage(g, g)
            with dve.Fori(4, NG - 3, 4) as g:
                for n in range(4):
                    stage(g + n, n)
            dve.wait_ge(f_st, NG)
            moments(NG - 1, 3)
            scale_bias(NG - 2, 2)
            scaled(NG - 2, 2)
            scale_bias(NG - 1, 3)
            scaled(NG - 1, 3)

        @block.gpsimd
        def _(pool):
            def halves():
                pool.wait_ge(con_in, 16)
                pool.wait_ge(w_in, 16)
                for g, un_ in enumerate(("uf", "ui", "uc")):
                    half = 0.5 if g < 2 else 1.0
                    pool.tensor_scalar(gate_u[:, g, :], w(un_), 0.5 * half, 1.0, ALU.mult, ALU.mult)
                pool.tensor_scalar(out_u[:], w("uo"), 0.5, 1.0, ALU.mult, ALU.mult).then_inc(prep_pool, 1)
                pool.wait_ge(front_lo, 1)

            def root(n, b):
                pool.wait_ge(mv_v[n], nth(b, 1, 1))
                pool.tensor_tensor(ve[n][:], mv[n][:, :, 1], ln_eps[:, min(n, 1), 0:T], ALU.add).then_inc(ve_p[n], 1)
                pool.wait_ge(ve_p[n], nth(b, 1, 1))
                pool.tensor_tensor(rstd[n][:], ve[n][:], minus_half[:, 0:T], ALU.pow).then_inc(rs_p[n], 1)

            def x_part(b):
                pool.wait_ge(xhi_a, nth(b, 1, 1))
                pool.tensor_tensor(x_lo[:], xT[:], x_hi[:].bitcast(F32), ALU.subtract).then_inc(xlo_p, 1)

            def keys(b):
                pool.wait_ge(k_a, nth(b, 1, 1))
                three_dims = "p (s n) -> p s n"
                pool.tensor_tensor(k_c[:].rearrange(three_dims, s=STEPS), k_two[:, 0:BT].rearrange(three_dims, s=STEPS),
                                   turned("k_cos"), ALU.mult)
                pool.tensor_tensor(k_s[:].rearrange(three_dims, s=STEPS),
                                   k_two[:, BT:2 * BT].rearrange(three_dims, s=STEPS),
                                   turned("k_sin"), ALU.mult).then_inc(kmul_p, 1)
                pool.wait_ge(kmul_p, nth(b, 1, 1))
                pool.tensor_tensor(kT[:], k_c[:], k_s[:], ALU.add).then_inc(k_p, 1)

            def keep_rows(b):
                pool.wait_ge(x2_v, nth(b, 1, 1))
                pool.tensor_copy(x2_all[:, bass.ds(b * BT, BT)],
                                 x2[:].rearrange("p t d -> p (t d)")).then_inc(keep_p, 1)

            def body(i):
                if isinstance(i, int) and i == 0:
                    x_part(0)
                    halves()
                if live(i - 2):
                    keys(i - 2)
                if live(i - 1):
                    b = i - 1
                    pool.wait_ge(xb_in, nth(b, 16, 16))
                    if live(b - 1):
                        pool.wait_ge(s1_v, nth(b - 1, 1, 1))
                    pool.tensor_tensor(x_mlp_b[:], x_mlp[:], w("b2").unsqueeze(1).broadcast_to([P, T, D]),
                                       ALU.add).then_inc(xb_p, 1)
                if live(i - 2):
                    pool.wait_ge(qmul_v, nth(i - 2, 1, 1))
                    pool.tensor_tensor(qT[:], q_c[:], q_s[:], ALU.add).then_inc(q_p, 1)
                if last_retention(i):
                    keep_rows(i - 3)
                if live(i - 1):
                    pool.wait_ge(chi_a, nth(i - 1, 1, 1))
                    pool.tensor_tensor(ctx_lo[:], ctxT[:], ctx_hi[:].bitcast(F32), ALU.subtract).then_inc(clo_p, 1)
                if not (isinstance(i, int) and not live(i + 1)):
                    x_part(i + 1)
                if live(i - 1):
                    root(1, i - 1)
                if live(i - 2):
                    root(2, i - 2)
                if live(i - 1):
                    pool.wait_ge(x1hi_a, nth(i - 1, 1, 1))
                    pool.tensor_tensor(x1_lo[:], x1T[:], x1_hi[:].bitcast(F32), ALU.subtract).then_inc(x1lo_p, 1)
                if live(i - 2):
                    pool.wait_ge(x2T_a, nth(i - 2, 1, 1))
                    pool.tensor_tensor(x2_lo[:], x2T_all[:, bass.ds((i - 2) * BT, BT)], x2_hi[:].bitcast(F32),
                                       ALU.subtract).then_inc(x2lo_p, 1)
                if live(i):
                    root(0, i)
                if live(i - 2) and not last_mlp(i):
                    keep_rows(i - 2)

            for i in range(LOOP0):
                body(i)
            with pool.Fori(LOOP0, AHEAD1 - U + 1, U) as i:
                for n in range(U):
                    body(i + n)
            for i in range(AHEAD1, LAST):
                body(i)

            def residual(g, odd):
                pool.wait_ge(f_tanh, g + 1)
                pool.tensor_tensor(group(x2_all, g, GT - 1, GT), group(x2_all, g, GT - 1, GT),
                                   e_h[:, odd, (GT - 1) * D:GT * D], ALU.add).then_inc(f_sp, 1)

            def rooted(g, n):
                pool.wait_ge(f_mv, g + 1)
                pool.tensor_tensor(e_ve[:, n, :], e_mv[:, n, :, 1], ln_eps[:, 1, :], ALU.add).then_inc(f_ve, 1)
                pool.wait_ge(f_ve, g + 1)
                pool.tensor_tensor(e_rs[:, n, :], e_ve[:, n, :], minus_half[:], ALU.pow).then_inc(f_rs, 1)

            pool.wait_ge(keep_p, NB)
            residual(0, 0)
            for g in range(1, 5):
                residual(g, g % 2)
                rooted(g - 1, g - 1)
            with pool.Fori(5, NG - 3, 4) as g:
                for n in range(4):
                    residual(g + n, (n + 1) % 2)
                    rooted(g + (n - 1), n)
            for g in range(NG - 3, NG):
                residual(g, g % 2)
                rooted(g - 1, (g - 1) % 4)
            rooted(NG - 1, 3)


def tables():
    f = np.float32
    pos = np.arange(SEQ, dtype=f)
    half = D // 2
    vec = (np.arange(0, D, 2, dtype=f) + f(0.4 * D)) / f(1.4 * D)
    scale = vec[None, :] ** (pos / f(SCALE_BASE))[:, None]
    freqs = f(1.0) / f(THETA) ** (np.arange(half, dtype=f) / f(half))
    angle = pos[:, None] * freqs[None, :]
    up = lambda a: np.repeat(a, 2, axis=-1).T.astype(f)
    sin, cos = np.sin(angle), np.cos(angle)
    inv = f(1.0) / scale
    r = np.arange(P)
    same = (r[:, None] // SEQ) == (r[None, :] // SEQ)
    later = same & (r[None, :] >= r[:, None])
    diff = (r[None, :] - r[:, None]).astype(f)
    return {"ident": np.eye(P), "causal": later, "decay": np.where(later, f(GAMMA) ** np.where(later, diff, 0), 0),
            "q_cos": up(cos * scale), "q_sin": up(sin * scale), "k_cos": up(cos * inv), "k_sin": up(sin * inv)}


def kernel(**inputs):
    import concourse.bacc as _bacc
    from concourse.bass_utils import run_bass_kernel_spmd as _run

    a = {k: np.asarray(v) for k, v in inputs.items()}
    blocks = lambda x: x.reshape(NB, T, P, D).transpose(0, 2, 1, 3).reshape(NB, P, T * D)
    columns = lambda x: x.reshape(NB, BT, D).transpose(0, 2, 1)
    om = a["L0_attn_omega"].T
    pack = {
        "aq_T": a["L0_attn_Wq"].T, "ak_T": a["L0_attn_Wk"].T, "av_T": a["L0_attn_Wv"].T, "ao": a["L0_attn_Wo"],
        "omega_T": np.concatenate([om, om], axis=0), "aq": a["L0_attn_Wq"], "ak": a["L0_attn_Wk"],
        "w1": a["L0_attn_W1"], "w2": a["L0_attn_W2"].reshape(FC, P, D).transpose(1, 0, 2).reshape(P, FC * D),
        "b1": a["L0_attn_b1"].reshape(FC, P).T, "gamma": a["L0_attn_gamma"][:, None],
        "beta": a["L0_attn_beta"][:, None], "b2": np.tile(a["L0_attn_b2"][None, :], (P, 1)),
        "rq": a["L0_xattn_Wq"], "rk": a["L0_xattn_Wk"], "rv": a["L0_xattn_Wv"],
        "wf": a["L0_ffn_wf"].T, "wi": a["L0_ffn_wi"].T, "wc": a["L0_ffn_wc"].T,
        "uf": a["L0_ffn_uf"].T, "ui": a["L0_ffn_ui"].T, "uc": a["L0_ffn_uc"].T,
        "wo": a["L0_ffn_wo"].T, "uo": a["L0_ffn_uo"].T, "c0": a["L0_ffn_in_c"][:, None],
        "gate_b": np.stack([a["L0_ffn_bf"], a["L0_ffn_bi"], a["L0_ffn_bc"]], axis=1),
    }
    made = tables()
    arrays = {
        "x_rows": blocks(a["x"]), "x_cols": columns(a["x"]), "ctx_cols": columns(a["ctx_1024"]),
        "weights": np.concatenate([pack[n] for n, _ in W_COLS], axis=1),
        "out_bias": a["L0_ffn_bo"][None, :],
        "consts": np.concatenate([made[n].astype(np.float32) for n, _ in C_COLS], axis=1),
    }
    arrays = {k: np.ascontiguousarray(v) for k, v in arrays.items()}
    nc = _bacc.Bacc("TRN2", target_bir_lowering=False, num_devices=1)
    args = [nc.dram_tensor(k, v.shape, F32, kind="ExternalInput").ap() for k, v in arrays.items()]
    out = nc.dram_tensor("out", (NG, P, GT * D), F32, kind="ExternalOutput").ap()
    program(nc, *args, out)
    r = _run(nc, [arrays], core_ids=[0])
    got = r.results[0]["out"]
    return got.reshape(NG, P, GT, D).transpose(0, 2, 1, 3).reshape(SEQS, SEQ, D)
```
